# Optimizing a Trainium2 kernel written in Bass

```python
import numpy as np
import jax
import jax.numpy as jnp

def _softmax(x, axis=-1):
    return jax.nn.softmax(x, axis=axis)

def _gelu(x):
    return jax.nn.gelu(x, approximate=True)

def _silu(x):
    return jax.nn.silu(x)

def _sigmoid(x):
    return jax.nn.sigmoid(x)

def _layernorm(x, axis=-1, eps=1e-05):
    m = jnp.mean(x, axis=axis, keepdims=True)
    v = jnp.var(x, axis=axis, keepdims=True)
    return (x - m) / jnp.sqrt(v + eps)

def _scatter_add(tgt, idx, src, axis=0):
    return tgt.at[idx].add(src)

def _segment_sum(src, seg, n):
    return jax.ops.segment_sum(src, seg, n)
kernel_name = 'mk_seq_preln_d1_jaxref_r8_21dcda'

def setup_inputs(seed: int=0):
    np.random.seed(seed)
    _w = jnp.asarray

    def _L0_attn_setup():
        import jax, jax.numpy as jnp
        import numpy as np
        D_MODEL = 128
        NUM_HEADS = 16
        HEAD_DIM = D_MODEL // NUM_HEADS
        THETA = 10000.0
        B, T = (4, 256)

        def _cos_sin(seq_len, head_dim, theta):
            freqs = 1.0 / theta ** (jnp.arange(0, head_dim, 2, dtype=jnp.float32) / head_dim)
            t = jnp.arange(seq_len, dtype=jnp.float32)
            angles = jnp.outer(t, freqs)
            return jnp.concatenate([jnp.cos(angles), jnp.sin(angles)], axis=-1)

        def _apply_rope(x, cos_sin):
            x1 = x[..., 0::2]
            x2 = x[..., 1::2]
            half = x.shape[-1] // 2
            cos = cos_sin[:, :half]
            sin = cos_sin[:, half:]
            out = jnp.stack([x1 * cos - x2 * sin, x1 * sin + x2 * cos], axis=-1)
            return out.reshape(x.shape)
        key = jax.random.key(seed)
        k1, k2, k3 = jax.random.split(key, 3)
        x = jax.random.normal(k1, (B, T, D_MODEL), dtype=jnp.float32)
        W_qkv = jax.random.normal(k2, (3 * D_MODEL, D_MODEL), dtype=jnp.float32) * D_MODEL ** (-0.5)
        W_out = jax.random.normal(k3, (D_MODEL, D_MODEL), dtype=jnp.float32) * D_MODEL ** (-0.5)
        return {'x': x, 'W_qkv': W_qkv, 'W_out': W_out}
    _L0_attn_in = _L0_attn_setup()

    def _L0_ffn_setup():
        import jax, jax.numpy as jnp
        import numpy as np
        DIM = 128
        DEPTH = 2
        HEADS = 8
        DIM_HEAD = 64
        WINDOW = 64
        INNER = HEADS * DIM_HEAD
        HID = int(DIM * 4 * 2 / 3)
        B, N = (2, 1024)
        QK_SCALE = 8.0

        def shift_token(t):
            t1, t2 = jnp.split(t, 2, axis=-1)
            t2 = jnp.pad(t2, ((0, 0), (1, 0), (0, 0)))[:, :-1]
            return jnp.concatenate([t1, t2], axis=-1)

        def l2norm(t):
            return t / jnp.clip(jnp.linalg.norm(t, axis=-1, keepdims=True), 1e-12)

        def rotate_half(x):
            x1, x2 = jnp.split(x, 2, axis=-1)
            return jnp.concatenate([-x2, x1], axis=-1)

        def rotary_xpos(q, k):
            n = q.shape[-2]
            half_idx = jnp.arange(0, DIM_HEAD, 2, dtype=jnp.float32)
            inv_freq = 1.0 / 10000.0 ** (half_idx / DIM_HEAD)
            t = jnp.arange(n, dtype=jnp.float32)
            freqs = t[:, None] * inv_freq[None, :]
            freqs = jnp.concatenate([freqs, freqs], axis=-1)
            base = (half_idx + 0.4 * DIM_HEAD) / (1.4 * DIM_HEAD)
            power = (t - n // 2) / float(WINDOW // 2)
            scale = base[None, :] ** power[:, None]
            scale = jnp.concatenate([scale, scale], axis=-1)
            cos, sin = (jnp.cos(freqs), jnp.sin(freqs))
            q = q * cos * scale + rotate_half(q) * sin * scale
            k = k * cos / scale + rotate_half(k) * sin / scale
            return (q, k)

        def local_attention(q, k, v):
            b, h, n, d = q.shape
            w = n // WINDOW
            bq = q.reshape(b, h, w, WINDOW, d) * QK_SCALE
            bk = k.reshape(b, h, w, WINDOW, d)
            bv = v.reshape(b, h, w, WINDOW, d)

            def look_around(t):
                p = jnp.pad(t, ((0, 0), (0, 0), (1, 0), (0, 0), (0, 0)))
                return jnp.concatenate([p[:, :, :w], p[:, :, 1:]], axis=3)
            bk, bv = (look_around(bk), look_around(bv))
            bt = jnp.arange(n).reshape(w, WINDOW)
            btp = jnp.pad(bt, ((1, 0), (0, 0)), constant_values=-1)
            btk = jnp.concatenate([btp[:w], btp[1:]], axis=1)
            sim = jnp.einsum('bhwid,bhwjd->bhwij', bq, bk)
            i = bt[:, :, None]
            j = btk[:, None, :]
            mask = (i < j) | (i > j + WINDOW) | (j == -1)
            sim = jnp.where(mask, -jnp.finfo(sim.dtype).max, sim)
            attn = jax.nn.softmax(sim, axis=-1)
            out = jnp.einsum('bhwij,bhwjd->bhwid', attn, bv)
            return out.reshape(b, h, n, d)

        def _layer(x, wqkv, qs, ksc, wo, lg, lb, w1, b1, w2, b2):
            b, n, _ = x.shape
            h = shift_token(x)
            qkv = h @ wqkv
            q, k, v = jnp.split(qkv, 3, axis=-1)
            to_heads = lambda t: t.reshape(b, n, HEADS, DIM_HEAD).transpose(0, 2, 1, 3)
            q, k, v = (to_heads(q), to_heads(k), to_heads(v))
            q = l2norm(q) * qs
            k = l2norm(k) * ksc
            q, k = rotary_xpos(q, k)
            o = local_attention(q, k, v)
            o = o.transpose(0, 2, 1, 3).reshape(b, n, INNER)
            x = x + o @ wo
            h = shift_token(x)
            mu = h.mean(-1, keepdims=True)
            var = h.var(-1, keepdims=True)
            h = (h - mu) / jnp.sqrt(var + 1e-05) * lg + lb
            h = h @ w1 + b1
            a, g = jnp.split(h, 2, axis=-1)
            h = a * jax.nn.gelu(g, approximate=False)
            x = x + h @ w2 + b2
            return x
        key = jax.random.key(seed)
        ks = jax.random.split(key, 6)
        return {'x': jax.random.normal(ks[0], (B, N, DIM), jnp.float32), 'wqkv': jax.random.normal(ks[1], (DEPTH, DIM, 3 * INNER), jnp.float32) * 0.02, 'q_scale': jnp.ones((DEPTH, DIM_HEAD), jnp.float32), 'k_scale': jnp.ones((DEPTH, DIM_HEAD), jnp.float32), 'wo': jax.random.normal(ks[2], (DEPTH, INNER, DIM), jnp.float32) * 0.02, 'ln_g': jnp.ones((DEPTH, DIM), jnp.float32), 'ln_b': jnp.zeros((DEPTH, DIM), jnp.float32), 'w1': jax.random.normal(ks[3], (DEPTH, DIM, 2 * HID), jnp.float32) * 0.02, 'b1': jnp.zeros((DEPTH, 2 * HID), jnp.float32), 'w2': jax.random.normal(ks[4], (DEPTH, HID, DIM), jnp.float32) * 0.02, 'b2': jnp.zeros((DEPTH, DIM), jnp.float32)}
    _L0_ffn_in = _L0_ffn_setup()
    _d = {'L0_attn_x': _L0_attn_in['x'], 'L0_attn_W_qkv': _L0_attn_in['W_qkv'], 'L0_attn_W_out': _L0_attn_in['W_out'], 'L0_ffn_wqkv': _L0_ffn_in['wqkv'], 'L0_ffn_q_scale': _L0_ffn_in['q_scale'], 'L0_ffn_k_scale': _L0_ffn_in['k_scale'], 'L0_ffn_wo': _L0_ffn_in['wo'], 'L0_ffn_ln_g': _L0_ffn_in['ln_g'], 'L0_ffn_ln_b': _L0_ffn_in['ln_b'], 'L0_ffn_w1': _L0_ffn_in['w1'], 'L0_ffn_b1': _L0_ffn_in['b1'], 'L0_ffn_w2': _L0_ffn_in['w2'], 'L0_ffn_b2': _L0_ffn_in['b2']}
    _x0 = _d['L0_attn_x']
    _d['L0_attn_x'] = jax.random.normal(jax.random.fold_in(jax.random.key(seed), 1), (32, 256, 128), dtype=_x0.dtype)
    del _x0
    return _d

def reference(L0_attn_x, L0_attn_W_qkv, L0_attn_W_out, L0_ffn_wqkv, L0_ffn_q_scale, L0_ffn_k_scale, L0_ffn_wo, L0_ffn_ln_g, L0_ffn_ln_b, L0_ffn_w1, L0_ffn_b1, L0_ffn_w2, L0_ffn_b2):

    def _L0_attn_ref(x, W_qkv, W_out):
        import jax, jax.numpy as jnp
        import numpy as np
        D_MODEL = 128
        NUM_HEADS = 16
        HEAD_DIM = D_MODEL // NUM_HEADS
        THETA = 10000.0
        B, T = (4, 256)

        def _cos_sin(seq_len, head_dim, theta):
            freqs = 1.0 / theta ** (jnp.arange(0, head_dim, 2, dtype=jnp.float32) / head_dim)
            t = jnp.arange(seq_len, dtype=jnp.float32)
            angles = jnp.outer(t, freqs)
            return jnp.concatenate([jnp.cos(angles), jnp.sin(angles)], axis=-1)

        def _apply_rope(x, cos_sin):
            x1 = x[..., 0::2]
            x2 = x[..., 1::2]
            half = x.shape[-1] // 2
            cos = cos_sin[:, :half]
            sin = cos_sin[:, half:]
            out = jnp.stack([x1 * cos - x2 * sin, x1 * sin + x2 * cos], axis=-1)
            return out.reshape(x.shape)
        Bsz, Tlen, _ = x.shape
        qkv = jnp.einsum('bti,oi->bto', x, W_qkv)
        qkv = qkv.reshape(Bsz, Tlen, 3 * NUM_HEADS, HEAD_DIM).transpose(0, 2, 1, 3)
        q, k, v = jnp.split(qkv, 3, axis=1)
        cos_sin = _cos_sin(Tlen, HEAD_DIM, THETA)
        q = _apply_rope(q, cos_sin)
        k = _apply_rope(k, cos_sin)
        scores = jnp.einsum('bhqd,bhkd->bhqk', q, k) / np.sqrt(HEAD_DIM).astype(np.float32)
        causal = jnp.tril(jnp.ones((Tlen, Tlen), dtype=bool))
        scores = jnp.where(causal[None, None], scores, -jnp.inf)
        attn = jax.nn.softmax(scores, axis=-1)
        o = jnp.einsum('bhqk,bhkd->bhqd', attn, v)
        o = o.transpose(0, 2, 1, 3).reshape(Bsz, Tlen, D_MODEL)
        return jnp.einsum('bti,oi->bto', o, W_out)

    def _L0_ffn_ref(x, wqkv, q_scale, k_scale, wo, ln_g, ln_b, w1, b1, w2, b2):
        import jax, jax.numpy as jnp
        import numpy as np
        DIM = 128
        DEPTH = 2
        HEADS = 8
        DIM_HEAD = 64
        WINDOW = 64
        INNER = HEADS * DIM_HEAD
        HID = int(DIM * 4 * 2 / 3)
        B, N = (2, 1024)
        QK_SCALE = 8.0

        def shift_token(t):
            t1, t2 = jnp.split(t, 2, axis=-1)
            t2 = jnp.pad(t2, ((0, 0), (1, 0), (0, 0)))[:, :-1]
            return jnp.concatenate([t1, t2], axis=-1)

        def l2norm(t):
            return t / jnp.clip(jnp.linalg.norm(t, axis=-1, keepdims=True), 1e-12)

        def rotate_half(x):
            x1, x2 = jnp.split(x, 2, axis=-1)
            return jnp.concatenate([-x2, x1], axis=-1)

        def rotary_xpos(q, k):
            n = q.shape[-2]
            half_idx = jnp.arange(0, DIM_HEAD, 2, dtype=jnp.float32)
            inv_freq = 1.0 / 10000.0 ** (half_idx / DIM_HEAD)
            t = jnp.arange(n, dtype=jnp.float32)
            freqs = t[:, None] * inv_freq[None, :]
            freqs = jnp.concatenate([freqs, freqs], axis=-1)
            base = (half_idx + 0.4 * DIM_HEAD) / (1.4 * DIM_HEAD)
            power = (t - n // 2) / float(WINDOW // 2)
            scale = base[None, :] ** power[:, None]
            scale = jnp.concatenate([scale, scale], axis=-1)
            cos, sin = (jnp.cos(freqs), jnp.sin(freqs))
            q = q * cos * scale + rotate_half(q) * sin * scale
            k = k * cos / scale + rotate_half(k) * sin / scale
            return (q, k)

        def local_attention(q, k, v):
            b, h, n, d = q.shape
            w = n // WINDOW
            bq = q.reshape(b, h, w, WINDOW, d) * QK_SCALE
            bk = k.reshape(b, h, w, WINDOW, d)
            bv = v.reshape(b, h, w, WINDOW, d)

            def look_around(t):
                p = jnp.pad(t, ((0, 0), (0, 0), (1, 0), (0, 0), (0, 0)))
                return jnp.concatenate([p[:, :, :w], p[:, :, 1:]], axis=3)
            bk, bv = (look_around(bk), look_around(bv))
            bt = jnp.arange(n).reshape(w, WINDOW)
            btp = jnp.pad(bt, ((1, 0), (0, 0)), constant_values=-1)
            btk = jnp.concatenate([btp[:w], btp[1:]], axis=1)
            sim = jnp.einsum('bhwid,bhwjd->bhwij', bq, bk)
            i = bt[:, :, None]
            j = btk[:, None, :]
            mask = (i < j) | (i > j + WINDOW) | (j == -1)
            sim = jnp.where(mask, -jnp.finfo(sim.dtype).max, sim)
            attn = jax.nn.softmax(sim, axis=-1)
            out = jnp.einsum('bhwij,bhwjd->bhwid', attn, bv)
            return out.reshape(b, h, n, d)

        def _layer(x, wqkv, qs, ksc, wo, lg, lb, w1, b1, w2, b2):
            b, n, _ = x.shape
            h = shift_token(x)
            qkv = h @ wqkv
            q, k, v = jnp.split(qkv, 3, axis=-1)
            to_heads = lambda t: t.reshape(b, n, HEADS, DIM_HEAD).transpose(0, 2, 1, 3)
            q, k, v = (to_heads(q), to_heads(k), to_heads(v))
            q = l2norm(q) * qs
            k = l2norm(k) * ksc
            q, k = rotary_xpos(q, k)
            o = local_attention(q, k, v)
            o = o.transpose(0, 2, 1, 3).reshape(b, n, INNER)
            x = x + o @ wo
            h = shift_token(x)
            mu = h.mean(-1, keepdims=True)
            var = h.var(-1, keepdims=True)
            h = (h - mu) / jnp.sqrt(var + 1e-05) * lg + lb
            h = h @ w1 + b1
            a, g = jnp.split(h, 2, axis=-1)
            h = a * jax.nn.gelu(g, approximate=False)
            x = x + h @ w2 + b2
            return x
        for l in range(DEPTH):
            x = _layer(x, wqkv[l], q_scale[l], k_scale[l], wo[l], ln_g[l], ln_b[l], w1[l], b1[l], w2[l], b2[l])
        return x
    x = L0_attn_x
    x = x + _L0_attn_ref(_layernorm(x, axis=-1), L0_attn_W_qkv, L0_attn_W_out)
    x = x + _L0_ffn_ref(_layernorm(x, axis=-1), L0_ffn_wqkv, L0_ffn_q_scale, L0_ffn_k_scale, L0_ffn_wo, L0_ffn_ln_g, L0_ffn_ln_b, L0_ffn_w1, L0_ffn_b1, L0_ffn_w2, L0_ffn_b2)
    return x

_drawn_inputs = setup_inputs


def setup_inputs(seed=0):
    import zlib

    import numpy as np

    out = dict(_drawn_inputs(seed))
    spreads = {'L0_ffn_q_scale': (1.0, 0.6),
     'L0_ffn_k_scale': (1.0, 0.6),
     'L0_ffn_ln_g': (1.0, 0.6),
     'L0_ffn_ln_b': (0.0, 0.8),
     'L0_ffn_b1': (0.0, 0.8),
     'L0_ffn_b2': (0.0, 0.508)}
    factors = {'L0_ffn_wqkv': 2.968, 'L0_ffn_wo': 2.966, 'L0_ffn_w1': 6.247, 'L0_ffn_w2': 6.156}
    for name, (base, spread) in spreads.items():
        noise = np.random.default_rng([zlib.crc32(name.encode()), seed]).standard_normal(out[name].shape)
        drawn = base * np.exp(spread * noise) if base else spread * noise
        out[name] = jnp.asarray(drawn.astype(out[name].dtype))
    for name, factor in factors.items():
        out[name] = (out[name] * factor).astype(out[name].dtype)
    return out
```

```python
import numpy as np

from contextlib import ExitStack

import concourse.bass as bass
from concourse import mybir

F32 = mybir.dt.float32
F32R = mybir.dt.float32r
BF16 = mybir.dt.bfloat16
ALU = mybir.AluOpType
ACT = mybir.ActivationFunctionType
AX = mybir.AxisListType

SEQS, T, D = 32, 256, 128
TILES = T // 128
EPS = 1e-5
MASKED = -1e30

HA, DA = 16, 8
CHUNKS = HA // 4
SCALE_A = float(np.float32(1.0) / np.sqrt(np.float32(DA)))

HB, DB, WINDOW = 8, 64, 64
NORM_MIN, NORM_SHIFT = 1e-12, 256.0
QK_SCALE = 8.0

HIDDEN = int(D * 4 * 2 / 3)
HC = 114

DEPTH = 2


def live(seq):
    return not isinstance(seq, int) or 0 <= seq < SEQS


def count(seq, per_seq, unit=0):
    return seq * per_seq + unit + 1


def landed(seq, parity):
    return seq * 8 + (16 - 8 * parity)


def build(nc, t, out):
    with ExitStack() as ctx:
        def sb(name, shape, dt=F32):
            return ctx.enter_context(nc.sbuf_tensor(name, shape, dt))

        banks = [ctx.enter_context(nc.psum_tensor(f"bank{i}", [128, 512], F32)) for i in range(8)]
        m = dict(
            xa=sb("xa", [128, SEQS * TILES, D]),
            z=sb("z", [128, SEQS * TILES, D]),
            ident=sb("ident", [128, 128]),
            identb=sb("identb", [128, 128], BF16),
            eps=sb("eps", [128, 1]),
        )
        attention_stage(nc, t, m, banks)
        m["half_stats"] = sb("half_stats", [128, 2, SEQS * TILES, 6])
        window = window_buffers(nc, ctx)
        mlp = mlp_buffers(nc, ctx)
        constants(nc, ctx, t, window, mlp)
        with nc.Fori(0, DEPTH) as layer:
            window_stage(nc, t, m, banks, window, layer)
            mlp_stage(nc, t, m, banks, mlp, layer, out)


def constants(nc, ctx, t, window, mlp):
    loaded = ctx.enter_context(nc.semaphore("const_loaded"))
    names = ("rope", "head_sum", "head_rep", "mask_q", "mask_k", "head_row")
    with nc.Block() as block:
        @block.sync
        def _(sp):
            for name in names:
                dst = window[name] if name == "head_rep" else window[name][:]
                sp.dma_start(dst, t["b_" + name]).then_inc(loaded, 16)
            sp.wait_ge(loaded, 16 * len(names))

        @block.gpsimd
        def _(pool):
            nc.gpsimd.memset(window["ones"][:], 1.0)

        @block.vector
        def _(dve):
            nc.vector.memset(window["hT"][64:128, 0:1], 0.0)
            dve.wait_ge(loaded, 16 * len(names))
            nc.vector.tensor_copy(window["head_rep_r"][:], window["head_rep"])
            nc.vector.memset(mlp["zeros"][:], 0.0)


def attention_stage(nc, t, m, banks):
    xa, z, ident, identb, eps = (m[k] for k in ("xa", "z", "ident", "identb", "eps"))
    with ExitStack() as ctx:
        def sb(name, shape, dt=F32):
            return ctx.enter_context(nc.sbuf_tensor("a_" + name, shape, dt))

        def sem(name):
            return ctx.enter_context(nc.semaphore("a_" + name))

        w_qk = sb("w_qk", [128, 4, 128])
        w_v = sb("w_v", [128, 128])
        w_out = sb("w_out", [128, CHUNKS, 128])
        rope_c = sb("rope_c", [128, 2, T])
        rope_s = sb("rope_s", [128, 2, T])
        mask_q = sb("mask_q", [128, 2, 128], BF16)
        max_rows = sb("max_rows", [3 * HA, CHUNKS, 128], BF16)
        k_ones = sb("k_ones", [128, 1])
        sel_raw = sb("sel_raw", [128, 16 * 128])
        sel = sb("sel", [128, 2, 2, CHUNKS, 128], F32R)
        ones = sb("ones", [128, 32])
        xn = sb("xn", [128, TILES, D])
        stats = sb("stats", [128, 2, 6])
        mean_var = sb("mean_var", [128, 2, 2])
        log_var = sb("log_var", [128, 2])
        rstd = sb("rstd", [128, 2])
        stats2 = sb("stats2", [128, 2, 6])
        mean_var2 = sb("mean_var2", [128, 2, 2])
        log_var2 = sb("log_var2", [128, 2])
        rstd2 = sb("rstd2", [128, 2])
        xT = [sb(f"xT{i}", [128, T]) for i in range(2)]
        rot_c = sb("rot_c", [128, 2, T])
        rot_s = sb("rot_s", [128, 2, T])
        qk = sb("qk", [128, 2, T])
        qk_hi = sb("qk_hi", [128, 2, T], F32R)
        qk_lo = sb("qk_lo", [128, 2, T], F32R)
        slots = [sb(f"slots{i}", [128, CHUNKS, 2, T], F32R) for i in range(2)]
        v = [sb(f"v{i}", [128, TILES, HA, 32]) for i in range(2)]
        neg_max3 = [sb(f"neg_max3_{i}", [128, HA, 3]) for i in range(2)]
        neg_max = sb("neg_max", [128, 2, HA])
        rest1 = sb("rest1", [128, 2, HA])
        rest2 = sb("rest2", [128, 2, HA])
        parts = sb("parts", [128, 2, 3 * HA], BF16)
        neg_maxT = [sb(f"neg_maxT{i}", [3 * HA, T], BF16) for i in range(2)]
        probs = sb("probs", [128, 8, 384])
        log_den = sb("log_den", [128, T])
        inv_den = sb("inv_den", [128, T])
        oT = sb("oT", [128, CHUNKS, T])
        bank_s, bank_p, bank_o, bank_m, bank_6, bank_7 = banks[0:2], banks[2:4], banks[4], banks[5], banks[6], banks[7]
        partsT = bank_m[:, 0:T // 2].bitcast(BF16)

        const_in = sem("const_in")
        x_in = [sem("x_in0"), sem("x_in1")]
        const_set = sem("const_set")
        sel_set = sem("sel_set")
        stats_set = sem("stats_set")
        mv_set = sem("mv_set")
        logv_set = sem("logv_set")
        rstd_set = sem("rstd_set")
        xn_set = sem("xn_set")
        stats2_set = sem("stats2_set")
        mv2_set = sem("mv2_set")
        logv2_set = sem("logv2_set")
        rstd2_set = sem("rstd2_set")
        z_set = sem("z_set")
        xT_mm = sem("xT_mm")
        xT_set = sem("xT_set")
        qk_mm = sem("qk_mm")
        swap_mm = sem("swap_mm")
        v_mm = sem("v_mm")
        v_set = sem("v_set")
        rot_c_set = sem("rot_c_set")
        rot_s_set = sem("rot_s_set")
        qk_set = sem("qk_set")
        hi_set = sem("hi_set")
        lo_set = sem("lo_set")
        sel_mm = sem("sel_mm")
        slots_set = sem("slots_set")
        s_mm = sem("s_mm")
        max_set = sem("max_set")
        m_step = sem("m_step")
        mT_mm = sem("mT_mm")
        mT_set = sem("mT_set")
        p_mm = sem("p_mm")
        mx_mm = sem("mx_mm")
        mx_set = sem("mx_set")
        p_exp = sem("p_exp")
        p_set = sem("p_set")
        o_mm = sem("o_mm")
        logd_set = sem("logd_set")
        invd_set = sem("invd_set")
        oT_set = sem("oT_set")
        out_mm = sem("out_mm")
        xa_set = sem("xa_set")
        dve_held, pe_held, pool_held = sem("dve_held"), sem("pe_held"), sem("pool_held")

        block = ctx.enter_context(nc.Block())
        x_tiles = t["L0_attn_x"].rearrange("n (t p) d -> n p t d", p=128)
        N_CONST = 11
        LAG = 6

        def e_head(p, k):
            return (p - 1, k - LAG) if k >= LAG else (p - 2, 16 - LAG + k)

        def rows(seq):
            return bass.ds(seq * TILES, TILES) if not isinstance(seq, int) else slice(seq * TILES, seq * TILES + TILES)

        def tile(buf, seq, i):
            return buf[:, seq * TILES + i, :]

        def periods(eng, period):
            for p in range(-2, 4):
                period(p, p % 2)
            with eng.Fori(2, (SEQS - 2) // 2) as i:
                for par in range(2):
                    period(i * 2 + par, par)
            for p in range(SEQS - 2, SEQS + 2):
                period(p, p % 2)

        @block.sync
        def _(sp):
            for name, dst in (("ident", ident[:]), ("identb", identb[:])):
                sp.dma_start(dst, t[name]).then_inc(const_in, 16)
            for name, dst in (("w_qk", w_qk[:]), ("w_v", w_v[:]), ("w_out", w_out[:]), ("rope_c", rope_c[:]),
                              ("rope_s", rope_s[:]), ("mask_q", mask_q[:]), ("max_rows", max_rows[:]), ("k_ones", k_ones[:]),
                              ("sel", sel_raw[:])):
                sp.dma_start(dst, t["a_" + name]).then_inc(const_in, 16)
            for s in range(2):
                sp.dma_start(xa[:, rows(s), :], x_tiles[s]).then_inc(x_in[s], 16)
            with sp.Fori(1, SEQS // 2) as i:
                for par in range(2):
                    s = i * 2 + par
                    sp.wait_ge(x_in[par], landed(s - 2, par))
                    sp.dma_start(xa[:, rows(s), :], x_tiles[bass.ds(s, 1)].rearrange("n p t d -> p (n t) d")).then_inc(x_in[par], 16)

        @block.gpsimd
        def _(pool):
            nc.gpsimd.memset(v[0][:], 0.0).then_inc(const_set, 1)
            nc.gpsimd.memset(v[1][:], 0.0).then_inc(const_set, 1)
            nc.gpsimd.memset(ones[:], 1.0).then_inc(const_set, 1)
            nc.gpsimd.memset(eps[:], EPS).then_inc(const_set, 1)

            def mask(s, h):
                pool.wait_ge(p_exp, count(s, 16, h))
                pool.sem_inc(pool_held, 1)
                diag = probs[:, h % 8, :].rearrange("p (a n) -> p a n", n=128)[:, 0:3:2, :]
                nc.gpsimd.affine_select(out=diag, in_=diag, pattern=[[0, 2], [1, 128]], compare_op=ALU.is_ge, fill=0.0,
                                        base=0, channel_multiplier=-1).then_inc(p_set, 1)

            def add_rotated(p):
                if live(p + 1):
                    pool.wait_ge(rot_c_set, count(p + 1, 1))
                    pool.wait_ge(rot_s_set, count(p + 1, 1))
                    if live(p):
                        pool.wait_ge(hi_set, count(p, 1))
                        pool.wait_ge(lo_set, count(p, 1))
                    nc.gpsimd.tensor_tensor(qk[:], rot_c[:], rot_s[:], ALU.add).then_inc(qk_set, 1)

            def low_part(p):
                if live(p + 1):
                    pool.wait_ge(hi_set, count(p + 1, 1))
                    pool.wait_ge(qk_set, count(p + 1, 1))
                    if live(p):
                        pool.wait_ge(sel_mm, count(p, 4, 3))
                    nc.gpsimd.tensor_tensor(qk_lo[:], qk[:], qk_hi[:].bitcast(F32), ALU.subtract).then_inc(lo_set, 1)

            def period(p, par):
                for k in range(16):
                    s, h = e_head(p, k)
                    if live(s):
                        mask(s, h)
                    if k == 8:
                        add_rotated(p)
                    if k == 10:
                        low_part(p)

            periods(pool, period)

        @block.tensor
        def _(pe):
            pe.wait_ge(const_in, 16 * N_CONST)
            pe.wait_ge(const_set, 4)
            pe.wait_ge(sel_set, 1)

            def transpose_x(s):
                pe.wait_ge(xn_set, count(s, 2, 1))
                if live(s - 2):
                    pe.wait_ge(v_set, count(s - 2, 1))
                elif live(s - 1):
                    pe.wait_ge(rot_s_set, count(s - 1, 1))
                for i in range(TILES):
                    last = nc.tensor.transpose(bank_7[:, i * 128:(i + 1) * 128], xn[:, i, :], ident[:])
                last.then_inc(xT_mm, 1)

            def project_qk(s, par):
                pe.wait_ge(xT_set, count(s, 1))
                if live(s - 1):
                    pe.wait_ge(slots_set, 2 * count(s - 1, 4, 2))
                for i in range(2):
                    last = nc.tensor.matmul(bank_6[:, i * T:(i + 1) * T], w_qk[:, i, :], xT[par][:], start=True, stop=True)
                last.then_inc(qk_mm, 1)

            def project_swapped(s, par):
                for i in range(2):
                    last = nc.tensor.matmul(bank_7[:, i * T:(i + 1) * T], w_qk[:, 2 + i, :], xT[par][:], start=True, stop=True)
                last.then_inc(swap_mm, 1)

            def project_v(s, par):
                if live(s + 1):
                    pe.wait_ge(rot_s_set, count(s + 1, 1))
                else:
                    pe.wait_ge(v_set, count(s - 1, 1))
                for i in range(TILES):
                    last = nc.tensor.matmul(bank_7[:, i * 128:(i + 1) * 128], xT[par][:, i * 128:(i + 1) * 128], w_v[:],
                                            start=True, stop=True)
                last.then_inc(v_mm, 1)

            def spread(s, c):
                pe.wait_ge(lo_set, count(s, 1))
                if c == 0:
                    pe.wait_ge(rot_c_set, count(s, 1))
                    if live(s - 1):
                        pe.wait_ge(slots_set, 2 * count(s - 1, 4, 3))
                else:
                    pe.wait_ge(slots_set, 2 * count(s, 4, c - 1))
                    if c == 3 and live(s + 1):
                        pe.wait_ge(rot_c_set, count(s + 1, 1))
                for i in range(2):
                    dst = bank_6[:, i * T:(i + 1) * T]
                    nc.tensor.matmul(dst, sel[:, i, 0, c, :], qk_hi[:, i, :], start=True, stop=False)
                    last = nc.tensor.matmul(dst, sel[:, i, 1, c, :], qk_lo[:, i, :], start=False, stop=True)
                last.then_inc(sel_mm, 1)

            def score(s, h, par):
                if h % 4 == 0:
                    pe.wait_ge(slots_set, 2 * count(s, 4, h // 4))
                if h >= 2 or live(s - 1):
                    pe.wait_ge(max_set, count(s, 16, h - 2))
                r = slice(32 * (h % 4), 32 * (h % 4) + 32)
                q, k, bank = slots[par][r, h // 4, 0, :], slots[par][r, h // 4, 1, :], bank_s[h % 2]
                nc.tensor.matmul(bank[:, 0:128], q[:, 0:128], k[:, 0:128], start=True, stop=False, skip_group_check=True)
                nc.tensor.matmul(bank[:, 128:384], q[:, 128:256], k[:, 0:256], start=False, stop=False, skip_group_check=True)
                diag = bank[:, 0:512].rearrange("p (a b) -> p a b", b=256)[:, :, 0:128]
                nc.tensor.matmul(diag, identb[:], mask_q[:], start=False, stop=True, skip_group_check=True).then_inc(s_mm, 1)

            def score_t(s, h, par):
                if h % 8 == 0:
                    pe.wait_ge(mx_set, count(s, 2, h // 8))
                if h >= 2 or live(s - 1):
                    pe.wait_ge(p_exp, count(s, 16, h - 2))
                r = slice(32 * (h % 4), 32 * (h % 4) + 32)
                q, k, bank = slots[par][r, h // 4, 0, :], slots[par][r, h // 4, 1, :], bank_p[h % 2]
                nc.tensor.matmul(bank[:, 0:256], k[:, 0:128], q[:, 0:256], start=True, stop=False, skip_group_check=True)
                nc.tensor.matmul(bank[:, 256:384], k[:, 128:256], q[:, 128:256], start=False, stop=True,
                                 skip_group_check=True).then_inc(p_mm, 1)

            def place_max(s, pair, par):
                if pair == 0:
                    pe.wait_ge(mT_set, count(s, 1))
                else:
                    pe.wait_ge(mx_set, count(s, 2, 0))
                for i in range(2):
                    last = nc.tensor.matmul(bank_m[:, i * T:(i + 1) * T], max_rows[:, 2 * pair + i, :], neg_maxT[par][:],
                                            start=True, stop=True)
                last.then_inc(mx_mm, 1)

            def weigh(s, c, par):
                pe.wait_ge(p_set, count(s, 16, 4 * c + 3))
                if c == 0:
                    pe.wait_ge(v_set, count(s, 1))
                if c > 0 or live(s - 1):
                    pe.wait_ge(oT_set, count(s, 4, c - 1))
                for half in range(2):
                    for kt in range(2):
                        for j in range(4):
                            h = 4 * c + j
                            lhs = v[par][:, kt, h, :] if half == 0 else ones[:]
                            dst = bank_o[32 * j:32 * j + 32, half * T + kt * 128:half * T + 256]
                            src = probs[:, h % 8, 0:256] if kt == 0 else probs[:, h % 8, 256:384]
                            last = nc.tensor.matmul(dst, lhs, src, start=(kt == 0), stop=(kt == 1), skip_group_check=True)
                last.then_inc(o_mm, 1)

            def transpose_max(s):
                pe.wait_ge(m_step, count(s, 7, 6))
                if live(s - 2):
                    pe.wait_ge(xa_set, count(s - 2, 1))
                elif live(s - 1):
                    pe.wait_ge(mx_set, count(s - 1, 2, 1))
                pe.sem_inc(pe_held, 1)
                for i in range(2):
                    last = nc.tensor.transpose(partsT[0:3 * HA, i * 128:(i + 1) * 128], parts[:, i, :], identb[:])
                last.then_inc(mT_mm, 1)

            def project_out(s):
                pe.wait_ge(oT_set, count(s, 4, 3))
                if live(s + 1):
                    pe.wait_ge(mx_set, count(s + 1, 2, 1))
                elif live(s - 1):
                    pe.wait_ge(xa_set, count(s - 1, 1))
                for i in range(TILES):
                    for c in range(CHUNKS):
                        last = nc.tensor.matmul(bank_m[:, i * 128:(i + 1) * 128], oT[:, c, i * 128:(i + 1) * 128],
                                                w_out[:, c, :], start=(c == 0), stop=(c == CHUNKS - 1))
                last.then_inc(out_mm, 1)

            def period(p, par):
                for k in range(16):
                    if live(p):
                        score(p, k, par)
                    s, h = e_head(p, k)
                    if live(s):
                        score_t(s, h, 1 - par if k >= LAG else par)
                    if k in (0, 3, 8) and live(p):
                        spread(p, 1 + (k + 1) // 4)
                    if k == 13 and live(p + 1):
                        spread(p + 1, 0)
                    if k == 12 and live(p - 1):
                        weigh(p - 1, 0, 1 - par)
                    if k in (0, 4, 8) and live(p - 2):
                        weigh(p - 2, 1 + k // 4, par)
                    if k == 2 and live(p - 1):
                        transpose_max(p - 1)
                    if k in (4, 7) and live(p - 1):
                        place_max(p - 1, k // 7, 1 - par)
                    if k == 12 and live(p - 2):
                        project_out(p - 2)
                    if live(p + 1):
                        if k == 1:
                            transpose_x(p + 1)
                        if k == 5:
                            project_qk(p + 1, 1 - par)
                        if k == 6:
                            project_swapped(p + 1, 1 - par)
                    if k == 10 and live(p):
                        project_v(p, par)

            periods(pe, period)

        @block.vector
        def _(dve):
            dve.wait_ge(const_in, 16 * N_CONST)
            nc.vector.tensor_copy(sel[:].rearrange("p a b c n -> p (a b c n)"), sel_raw[:]).then_inc(sel_set, 1)

            def norm_stats(s, st, mv, st_sem, mv_sem, done):
                dve.sem_inc(dve_held, 1)
                for i in range(TILES):
                    nc.vector.bn_stats(st[:, i, :], tile(xa, s, i)).then_inc(st_sem, 1)
                if live(s - 1):
                    dve.wait_ge(done, count(s - 1, 2, 1))
                for i in range(TILES):
                    dve.wait_ge(st_sem, count(s, 2, i))
                    dve.sem_inc(dve_held, 1)
                    nc.vector.bn_aggr(mv[:, i, :], st[:, i, :]).then_inc(mv_sem, 1)

            def norm_apply(s, dst, mv, rs, dst_sem):
                for i in range(TILES):
                    nc.vector.tensor_scalar(dst(i), tile(xa, s, i), mv[:, i, 0:1], rs[:, i:i + 1],
                                            ALU.subtract, ALU.mult).then_inc(dst_sem, 1)

            def row_max(s, h, par):
                dve.wait_ge(s_mm, count(s, 16, h))
                nc.vector.tensor_reduce(neg_max3[par][:, h, :], bank_s[h % 2][:, 0:384].rearrange("p (b k) -> p b k", b=3),
                                        AX.X, ALU.max, negate=True).then_inc(max_set, 1)

            def cut_max(s, par):
                three = neg_max3[par]
                dve.wait_ge(max_set, count(s, 16, 15))
                if live(s - 1):
                    dve.wait_ge(m_step, count(s - 1, 7, 6))
                nc.vector.tensor_copy(neg_max[:, 0, :], three[:, :, 0]).then_inc(m_step, 1)
                nc.vector.tensor_tensor(neg_max[:, 1, :], three[:, :, 1], three[:, :, 2], ALU.min).then_inc(m_step, 1)
                dve.wait_ge(m_step, count(s, 7, 1))
                if live(s - 1):
                    dve.wait_ge(mT_mm, count(s - 1, 1))
                nc.vector.tensor_copy(parts[:, :, 0:HA], neg_max[:]).then_inc(m_step, 1)
                dve.wait_ge(m_step, count(s, 7, 2))
                nc.vector.tensor_tensor(rest1[:], neg_max[:], parts[:, :, 0:HA], ALU.subtract).then_inc(m_step, 1)
                dve.wait_ge(m_step, count(s, 7, 3))
                nc.vector.tensor_copy(parts[:, :, HA:2 * HA], rest1[:]).then_inc(m_step, 1)
                dve.wait_ge(m_step, count(s, 7, 4))
                nc.vector.tensor_tensor(rest2[:], rest1[:], parts[:, :, HA:2 * HA], ALU.subtract).then_inc(m_step, 1)
                dve.wait_ge(m_step, count(s, 7, 5))
                nc.vector.tensor_copy(parts[:, :, 2 * HA:3 * HA], rest2[:]).then_inc(m_step, 1)

            def set_max(s, par):
                dve.wait_ge(mT_mm, count(s, 1))
                if live(s - 2):
                    dve.wait_ge(mx_mm, count(s - 2, 2, 1))
                nc.vector.tensor_copy(neg_maxT[par][:], partsT[0:3 * HA, :]).then_inc(mT_set, 1)

            def add_max(s, pair, par):
                dve.wait_ge(mx_mm, count(s, 2, pair))
                q = slots[par][:, 2 * pair:2 * pair + 2, 0, :]
                nc.vector.tensor_tensor(q, q.bitcast(F32), bank_m[:].rearrange("p (a t) -> p a t", a=2), ALU.add).then_inc(mx_set, 1)

            def normalize(s, c):
                dve.wait_ge(invd_set, count(s, 4, c))
                if c == 0 and live(s - 1):
                    dve.wait_ge(out_mm, count(s - 1, 1))
                nc.vector.tensor_tensor(oT[:, c, :], bank_o[:, 0:T], inv_den[:], ALU.mult).then_inc(oT_set, 1)

            def period(p, par):
                for k in range(16):
                    if k == 3 and live(p - 1):
                        set_max(p - 1, 1 - par)
                    if k in (5, 8) and live(p - 1):
                        add_max(p - 1, k // 8, 1 - par)
                    if live(p):
                        row_max(p, k, par)
                    if k == 0 and live(p - 1):
                        cut_max(p - 1, 1 - par)
                    if k == 6 and live(p + 1):
                        dve.wait_ge(qk_mm, count(p + 1, 1))
                        if live(p):
                            dve.wait_ge(qk_set, count(p, 1))
                        nc.vector.tensor_tensor(rot_c[:], bank_6[:].rearrange("p (a t) -> p a t", a=2), rope_c[:],
                                                ALU.mult).then_inc(rot_c_set, 1)
                    if k == 7 and live(p + 1):
                        dve.wait_ge(swap_mm, count(p + 1, 1))
                        nc.vector.tensor_tensor(rot_s[:], bank_7[:].rearrange("p (a t) -> p a t", a=2), rope_s[:],
                                                ALU.mult).then_inc(rot_s_set, 1)
                    if k == 13 and live(p - 1):
                        normalize(p - 1, 0)
                    if k in (1, 5, 9) and live(p - 2):
                        normalize(p - 2, 1 + k // 4)
                    if k == 13 and live(p - 2):
                        dve.wait_ge(out_mm, count(p - 2, 1))
                        nc.vector.tensor_tensor(xa[:, rows(p - 2), :], xa[:, rows(p - 2), :],
                                                bank_m[:, 0:T].rearrange("p (t d) -> p t d", d=D), ALU.add).then_inc(xa_set, 1)
                    if k == 14 and live(p - 2):
                        dve.wait_ge(xa_set, count(p - 2, 1))
                        norm_stats(p - 2, stats2, mean_var2, stats2_set, mv2_set, z_set)
                    if k == 8 and live(p + 2):
                        dve.wait_ge(x_in[par], landed(p + 2, par))
                        norm_stats(p + 2, stats, mean_var, stats_set, mv_set, xn_set)
                    if k == 15 and live(p - 2):
                        dve.wait_ge(rstd2_set, count(p - 2, 1))
                        norm_apply(p - 2, lambda i: tile(z, p - 2, i), mean_var2, rstd2, z_set)
                    if k == 11 and live(p + 2):
                        dve.wait_ge(rstd_set, count(p + 2, 1))
                        if live(p + 1):
                            dve.wait_ge(xT_mm, count(p + 1, 1))
                        norm_apply(p + 2, lambda i: xn[:, i, :], mean_var, rstd, xn_set)

            periods(dve, period)

        @block.scalar
        def _(act):
            nc.scalar.preload_act_table_set("natural_log_exp_and_others")
            act.wait_ge(const_set, 4)

            def rsqrt_var(s, mv, lv, rs, mv_sem, lv_sem, rs_sem, used):
                act.wait_ge(mv_sem, count(s, 2, 1))
                if live(s - 1):
                    act.wait_ge(rs_sem, count(s - 1, 1))
                nc.scalar.activation(lv[:], mv[:, :, 1], ACT.Ln, bias=eps[:, 0:1]).then_inc(lv_sem, 1)
                act.wait_ge(lv_sem, count(s, 1))
                if live(s - 1):
                    act.wait_ge(used, count(s - 1, 2, 1))
                nc.scalar.activation(rs[:], lv[:], ACT.Exp, scale=-0.5).then_inc(rs_sem, 1)

            def exp_head(s, h):
                act.wait_ge(p_mm, count(s, 16, h))
                if h % 4 == 0 and (h >= 8 or live(s - 1)):
                    act.wait_ge(o_mm, count(s, 4, h // 4 - 2))
                nc.scalar.activation(probs[:, h % 8, :], bank_p[h % 2][:, 0:384], ACT.Exp, scale=SCALE_A).then_inc(p_exp, 1)

            def invert_den(s, c):
                act.wait_ge(o_mm, count(s, 4, c))
                if c > 0 or live(s - 1):
                    act.wait_ge(invd_set, count(s, 4, c - 1))
                nc.scalar.activation(log_den[:], bank_o[:, T:2 * T], ACT.Ln).then_inc(logd_set, 1)
                act.wait_ge(logd_set, count(s, 4, c))
                if c > 0 or live(s - 1):
                    act.wait_ge(oT_set, count(s, 4, c - 1))
                nc.scalar.activation(inv_den[:], log_den[:], ACT.Exp, scale=-1.0).then_inc(invd_set, 1)

            def set_slots(s, c, par):
                act.wait_ge(sel_mm, count(s, 4, c))
                if live(s - 2):
                    act.wait_ge(p_mm, count(s - 2, 16, 4 * c + 3))
                nc.scalar.activation(slots[par][:, c, 0, :], bank_6[:, 0:T], ACT.Copy).then_inc(slots_set, 1)
                nc.scalar.activation(slots[par][:, c, 1, :], bank_6[:, T:2 * T], ACT.Identity, bias=k_ones[:, 0:1]
                                     ).then_inc(slots_set, 1)

            def period(p, par):
                for k in range(16):
                    s, h = e_head(p, k)
                    if live(s):
                        exp_head(s, h)
                    if k in (0, 3, 8) and live(p):
                        set_slots(p, 1 + (k + 1) // 4, par)
                    if k == 13 and live(p + 1):
                        set_slots(p + 1, 0, 1 - par)
                    if k == 10 and live(p):
                        act.wait_ge(v_mm, count(p, 1))
                        if live(p - 2):
                            act.wait_ge(o_mm, count(p - 2, 4, 3))
                        nc.scalar.activation(v[par][:, :, :, 0:DA],
                                             bank_7[:, 0:T].rearrange("p (t h d) -> p t h d", t=2, d=DA),
                                             ACT.Copy).then_inc(v_set, 1)
                    if k == 12 and live(p - 1):
                        invert_den(p - 1, 0)
                    if k in (0, 4, 8) and live(p - 2):
                        invert_den(p - 2, 1 + k // 4)
                    if k == 1 and live(p + 1):
                        act.wait_ge(xT_mm, count(p + 1, 1))
                        if live(p - 1):
                            act.wait_ge(v_mm, count(p - 1, 1))
                        nc.scalar.activation(xT[1 - par][:], bank_7[:, 0:T], ACT.Copy).then_inc(xT_set, 1)
                    if k == 10 and live(p + 1):
                        act.wait_ge(qk_set, count(p + 1, 1))
                        if live(p):
                            act.wait_ge(sel_mm, count(p, 4, 3))
                        nc.scalar.activation(qk_hi[:], qk[:], ACT.Copy).then_inc(hi_set, 1)
                    if k == 15 and live(p - 2):
                        rsqrt_var(p - 2, mean_var2, log_var2, rstd2, mv2_set, logv2_set, rstd2_set, z_set)
                    if k == 9 and live(p + 2):
                        rsqrt_var(p + 2, mean_var, log_var, rstd, mv_set, logv_set, rstd_set, xn_set)

            periods(act, period)


def window_stage(nc, t, m, banks, w, layer):
    z, ident, identb = m["z"], m["ident"], m["identb"]
    bank_s, bank_p, bank_o, bank_m, bank_6, bank_7 = banks[0:2], banks[2:4], banks[4], banks[5], banks[6], banks[7]
    partsT = bank_m[:, 0:T // 2].bitcast(BF16)
    g = w
    s_ = w["sems"]

    def count(seq, per_seq, unit=0):
        return (layer * SEQS + seq) * per_seq + unit + 1

    def periods(eng, period):
        for p in range(-2, 4):
            period(p, p % 2)
        with eng.Fori(2, (SEQS - 2) // 2) as i:
            for par in range(2):
                period(i * 2 + par, par)
        for p in range(SEQS - 2, SEQS + 2):
            period(p, p % 2)

    def rows(seq):
        return bass.ds(seq * TILES, TILES) if not isinstance(seq, int) else slice(seq * TILES, seq * TILES + TILES)

    def e_head(p, k):
        return (p - 1, k - 2) if k >= 2 else (p - 2, 6 + k)

    UNITS = ("q heads 0-3", "k heads 0-3", "q heads 4-7", "k heads 4-7")

    with nc.Block() as block:
        @block.sync
        def _(sp):
            for name in ("w_qk", "w_v", "w_o", "scales"):
                sp.dma_start(g[name] if name in ("w_qk", "w_v") else g[name][:], t["b_" + name][bass.ds(layer, 1)].rearrange("l p n -> p (l n)")).then_inc(s_["w_in"], 16)

        @block.gpsimd
        def _(pool):
            def period(p, par):
                for k in range(8):
                    s, u = (p + 1, k // 2 + 1) if k < 6 else (p + 2, 0)
                    if k % 2 == 0 and live(s):
                        pool.wait_ge(s_["rot"], count(s, 8, 2 * u + 1))
                        if live(s - 1):
                            pool.wait_ge(s_["normed"], count(s - 1, 4, u))
                        for half in range(2):
                            nc.gpsimd.tensor_tensor(g["unit"][u][:, half, :], g["rot_c"][u % 2][:, half, :],
                                                    g["rot_s"][u % 2][:, 1 - half, :], ALU.add).then_inc(s_["summed"], 1)
                    if k == 1 and live(p + 2):
                        if live(p + 1):
                            pool.wait_ge(s_["hT_mm"], count(p + 1, 1))
                        pool.sem_inc(s_["pool_held"], 1)
                        nc.gpsimd.tensor_copy(g["z_in"][:], z[:, rows(p + 2), :]).then_inc(s_["z_in"], 1)
                    if k == 4 and live(p + 2):
                        pool.wait_ge(s_["hT_hi"], count(p + 2, 1))
                        if live(p):
                            pool.wait_ge(s_["v_mm"], count(p, 2, 1))
                        nc.gpsimd.tensor_tensor(g["hT_lo"][par][:], g["hT"][:], g["hT_hi"][par][:].bitcast(F32),
                                                ALU.subtract).then_inc(s_["hT_lo"], 1)
                    if k == 5 and live(p + 1):
                        pool.wait_ge(s_["rn_hi"], count(p + 1, 1))
                        if live(p):
                            pool.wait_ge(s_["rep_mm"], count(p, 2, 1))
                        nc.gpsimd.tensor_tensor(g["rn_lo"][:], g["rn"][:], g["rn_hi"][:].bitcast(F32),
                                                ALU.subtract).then_inc(s_["rn_lo"], 1)

            periods(pool, period)

        @block.tensor
        def _(pe):
            pe.wait_ge(s_["w_in"], 64 * (layer + 1))
            pe.wait_ge(s_["w_lo"], 2 * (layer + 1))

            def transpose_z(s):
                pe.wait_ge(s_["z_in"], count(s, 1))
                if live(s - 3):
                    pe.wait_ge(s_["mT"], count(s - 3, 1))
                elif live(s - 2):
                    pe.wait_ge(s_["ssq"], count(s - 2, 1))
                elif live(s - 1):
                    pe.wait_ge(s_["hT_psum"], count(s - 1, 2, 1))
                for i in range(TILES):
                    last = nc.tensor.transpose(bank_m[:, i * 128:(i + 1) * 128], g["z_in"][:, i, :], ident[:])
                last.then_inc(s_["hT_mm"], 1)

            def project_qk(s, u, par):
                if u == 0:
                    pe.wait_ge(s_["hT_lo"], count(s, 1))
                if u > 0 or live(s - 1):
                    pe.wait_ge(s_["rot"], count(s, 8, 2 * u - 1))
                for half in range(2):
                    dst, c = bank_6[:, half * T:(half + 1) * T], slice((2 * u + half) * 128, (2 * u + half + 1) * 128)
                    nc.tensor.matmul(dst, g["w_qk_hi"][:, c], g["hT_hi"][par][:], start=True, stop=False)
                    nc.tensor.matmul(dst, g["w_qk_hi"][:, c], g["hT_lo"][par][:], start=False, stop=False)
                    last = nc.tensor.matmul(dst, g["w_qk_lo"][:, c], g["hT_hi"][par][:], start=False, stop=True)
                last.then_inc(s_["qk_mm"], 1)

            def project_v(s, i, par):
                if i == 0:
                    pe.wait_ge(s_["normed"], count(s, 4, 3))
                if i == 1:
                    pe.wait_ge(s_["v"], count(s, 2, 0))
                hi, lo = (g[part][par][:, i * 128:(i + 1) * 128] for part in ("hT_hi", "hT_lo"))
                nc.tensor.matmul(bank_7[:], hi, g["w_v_hi"][:], start=True, stop=False)
                nc.tensor.matmul(bank_7[:], hi, g["w_v_lo"][:], start=False, stop=False)
                nc.tensor.matmul(bank_7[:], lo, g["w_v_hi"][:], start=False, stop=True).then_inc(s_["v_mm"], 1)

            def sum_squares(s):
                pe.wait_ge(s_["squares"], count(s, 4, 3))
                if live(s + 1):
                    pe.wait_ge(s_["hT_psum"], count(s + 1, 2, 1))
                else:
                    pe.wait_ge(s_["mT"], count(s - 2, 1))
                for half in range(2):
                    for u in range(4):
                        last = nc.tensor.matmul(bank_m[32 * u:32 * u + 32, 0:T], g["head_sum"][:], g["sq"][u][:, half, :],
                                                start=(half == 0), stop=(half == 1), skip_group_check=True)
                last.then_inc(s_["ssq_mm"], 1)

            def repeat_norms(s, pair):
                pe.wait_ge(s_["rn_lo"], count(s, 1))
                if pair == 1:
                    pe.wait_ge(s_["normed"], count(s, 4, 1))
                elif live(s - 1):
                    pe.wait_ge(s_["v"], count(s - 1, 2, 1))
                for i in range(2):
                    dst, rep = bank_7[:, i * T:(i + 1) * T], g["head_rep_r"][:, (2 * pair + i) * 128:(2 * pair + i + 1) * 128]
                    nc.tensor.matmul(dst, rep, g["rn_hi"][:], start=True, stop=False)
                    last = nc.tensor.matmul(dst, rep, g["rn_lo"][:], start=False, stop=True)
                last.then_inc(s_["rep_mm"], 1)

            def score(s, h, par):
                if h % 4 == 0:
                    pe.wait_ge(s_["moved"][h // 4], count(s, 8, 7))
                if h >= 2 or live(s - 1):
                    pe.wait_ge(s_["max"], 2 * count(s, 8, h - 2))
                r = slice(64 * (h % 2), 64 * (h % 2) + 64)
                q, k, bank = g["heads"][par][r, 0, h // 2, :], g["heads"][par][r, 1, h // 2, :], bank_s[h % 2]
                nc.tensor.matmul(bank[:, 0:128], q[:, 0:128], k[:, 0:128], start=True, stop=False, skip_group_check=True)
                nc.tensor.matmul(bank[:, 128:320], q[:, 128:256], k[:, 64:256], start=False, stop=False, skip_group_check=True)
                nc.tensor.matmul(bank[:, 0:320], identb[:], g["mask_q"][:], start=False, stop=True,
                                 skip_group_check=True).then_inc(s_["s_mm"], 1)

            def score_t(s, h, par):
                if h == 0:
                    pe.wait_ge(s_["mT"], count(s, 1))
                if h >= 2 or live(s - 1):
                    pe.wait_ge(s_["p"], count(s, 8, h - 2))
                r = slice(64 * (h % 2), 64 * (h % 2) + 64)
                q, k, bank = g["heads"][par][r, 0, h // 2, :], g["heads"][par][r, 1, h // 2, :], bank_p[h % 2]
                nm = g["neg_maxT"][par]
                nc.tensor.matmul(bank[:, 0:192], k[:, 0:128], q[:, 0:192], start=True, stop=False, skip_group_check=True)
                nc.tensor.matmul(bank[:, 192:320], k[:, 128:256], q[:, 128:256], start=False, stop=False, skip_group_check=True)
                nc.tensor.matmul(bank[:, 0:192], g["head_row"][:, h, :], nm[:, 0:192], start=False, stop=False, skip_group_check=True)
                nc.tensor.matmul(bank[:, 192:320], g["head_row"][:, h, :], nm[:, 128:256], start=False, stop=False, skip_group_check=True)
                nc.tensor.matmul(bank[:, 0:320], identb[:], g["mask_k"][:], start=False, stop=True,
                                 skip_group_check=True).then_inc(s_["p_mm"], 1)

            def weigh(s, c, par):
                pe.wait_ge(s_["p"], count(s, 8, 2 * c + 1))
                if c == 0:
                    pe.wait_ge(s_["v"], count(s, 2, 1))
                if c > 0 or live(s - 1):
                    pe.wait_ge(s_["oT"], count(s, 4, c - 1))
                for right in range(2):
                    for kt in range(2):
                        for a in range(2):
                            h = 2 * c + a
                            lhs = g["ones"][:] if right else g["v"][par][:, kt, h * DB:(h + 1) * DB]
                            dst = bank_o[64 * a:64 * a + 64, right * T + (128 if kt else 0):right * T + (256 if kt else 192)]
                            src = g["probs"][:, h % 4, 192:320] if kt else g["probs"][:, h % 4, 0:192]
                            last = nc.tensor.matmul(dst, lhs, src, start=(kt == 0), stop=(kt == 1), skip_group_check=True)
                last.then_inc(s_["o_mm"], 1)

            def transpose_max(s):
                pe.wait_ge(s_["cut"], count(s, 5, 4))
                if live(s - 2):
                    pe.wait_ge(s_["z_set"], count(s - 2, 1))
                elif live(s + 1):
                    pe.wait_ge(s_["ssq"], count(s + 1, 1))
                pe.sem_inc(s_["pe_held"], 1)
                for i in range(2):
                    last = nc.tensor.transpose(partsT[0:3 * HB, i * 128:(i + 1) * 128], g["parts"][:, i, :], identb[:])
                last.then_inc(s_["mT_mm"], 1)

            def project_out(s, i, par):
                pe.wait_ge(s_["oT"], count(s, 4, 3))
                if i == 1:
                    pass
                elif live(s + 3):
                    pe.wait_ge(s_["ssq"], count(s + 3, 1))
                elif live(s + 1):
                    pe.wait_ge(s_["mT"], count(s + 1, 1))
                elif live(s - 1):
                    pe.wait_ge(s_["z_set"], count(s - 1, 1))
                for c in range(4):
                    last = nc.tensor.matmul(bank_m[:, i * 128:(i + 1) * 128], g["oT"][par][:, c, i * 128:(i + 1) * 128],
                                            g["w_o"][:, c * D:(c + 1) * D], start=(c == 0), stop=(c == 3))
                last.then_inc(s_["out_mm"], 1)

            def period(p, par):
                for k in range(8):
                    if live(p):
                        score(p, k, par)
                    s, h = e_head(p, k)
                    if live(s):
                        score_t(s, h, 1 - par if k >= 2 else par)
                    if k == 4 and live(p + 1):
                        sum_squares(p + 1)
                    if k in (0, 2) and live(p - 2):
                        weigh(p - 2, 2 + k // 2, par)
                    if k in (4, 6) and live(p - 1):
                        weigh(p - 1, k // 2 - 2, 1 - par)
                    if k in (1, 3) and live(p + 1):
                        project_qk(p + 1, 2 + k // 2, 1 - par)
                    if k in (2, 3) and live(p):
                        project_v(p, k - 2, par)
                    if k == 0 and live(p):
                        repeat_norms(p, 1)
                    if k == 0 and live(p - 1):
                        transpose_max(p - 1)
                    if k == 3 and live(p + 2):
                        transpose_z(p + 2)
                    if k in (5, 7) and live(p + 2):
                        project_qk(p + 2, k // 2 - 2, par)
                    if k == 5 and live(p + 1):
                        repeat_norms(p + 1, 0)
                    if k in (6, 7) and live(p - 2):
                        project_out(p - 2, k - 6, par)

            periods(pe, period)

        @block.vector
        def _(dve):
            dve.wait_ge(s_["w_in"], 64 * (layer + 1))
            for side in range(2):
                for half in range(2):
                    sc = g["scales"][:, 2 * side + half:2 * side + half + 1]
                    nc.vector.tensor_scalar(g["tab_c"][:, side, half, :], g["rope"][:, side, 0, :], sc, None,
                                            ALU.mult).then_inc(s_["tables"], 1)
                    nc.vector.tensor_scalar(g["tab_s"][:, side, half, :], g["rope"][:, side, 1, :], sc, -1.0 if half else 1.0,
                                            ALU.mult, ALU.mult).then_inc(s_["tables"], 1)
            dve.wait_ge(s_["w_hi"], 2 * (layer + 1))
            for name in ("w_qk", "w_v"):
                nc.vector.tensor_tensor(g[name + "_lo"][:], g[name], g[name + "_hi"][:].bitcast(F32),
                                        ALU.subtract).then_inc(s_["w_lo"], 1)
            dve.wait_ge(s_["tables"], 8 * (layer + 1))

            def row_max(s, h, par):
                dve.wait_ge(s_["s_mm"], count(s, 8, h))
                nc.vector.tensor_reduce(g["neg_max"][par][:, 0, h:h + 1], bank_s[h % 2][:, 0:128], AX.X, ALU.max,
                                        negate=True).then_inc(s_["max"], 1)
                nc.vector.tensor_reduce(g["neg_max"][par][:, 1, h:h + 1], bank_s[h % 2][:, 128:320], AX.X, ALU.max,
                                        negate=True).then_inc(s_["max"], 1)

            def cut_max(s, par):
                nm, parts, rest = g["neg_max"][par], g["parts"], g["rest"]
                dve.wait_ge(s_["max"], 2 * count(s, 8, 7))
                if live(s - 1):
                    dve.wait_ge(s_["mT_mm"], count(s - 1, 1))
                nc.vector.tensor_copy(parts[:, :, 0:HB], nm[:]).then_inc(s_["cut"], 1)
                dve.wait_ge(s_["cut"], count(s, 5, 0))
                nc.vector.tensor_tensor(rest[0][:], nm[:], parts[:, :, 0:HB], ALU.subtract).then_inc(s_["cut"], 1)
                dve.wait_ge(s_["cut"], count(s, 5, 1))
                nc.vector.tensor_copy(parts[:, :, HB:2 * HB], rest[0][:]).then_inc(s_["cut"], 1)
                dve.wait_ge(s_["cut"], count(s, 5, 2))
                nc.vector.tensor_tensor(rest[1][:], rest[0][:], parts[:, :, HB:2 * HB], ALU.subtract).then_inc(s_["cut"], 1)
                dve.wait_ge(s_["cut"], count(s, 5, 3))
                nc.vector.tensor_copy(parts[:, :, 2 * HB:3 * HB], rest[1][:]).then_inc(s_["cut"], 1)

            def set_max(s, par):
                dve.wait_ge(s_["mT_mm"], count(s, 1))
                if live(s - 2):
                    dve.wait_ge(s_["p_mm"], count(s - 2, 8, 7))
                nc.vector.tensor_copy(g["neg_maxT"][par][:], partsT[0:3 * HB, :]).then_inc(s_["mT"], 1)

            def rotate(s, u):
                dve.wait_ge(s_["squares"], count(s, 4, u))
                if u >= 2 or live(s - 1):
                    dve.wait_ge(s_["summed"], 2 * count(s, 4, u - 2))
                src = bank_6[:].rearrange("p (a t) -> p a t", a=2)
                nc.vector.tensor_tensor(g["rot_c"][u % 2][:], src, g["tab_c"][:, u % 2], ALU.mult).then_inc(s_["rot"], 1)
                nc.vector.tensor_tensor(g["rot_s"][u % 2][:], src, g["tab_s"][:, u % 2], ALU.mult).then_inc(s_["rot"], 1)

            def clip_squares(s):
                dve.wait_ge(s_["ssq_mm"], count(s, 1))
                if live(s - 1):
                    dve.wait_ge(s_["log_norm"], count(s - 1, 1))
                nc.vector.tensor_scalar(g["ssq"][:], bank_m[:, 0:T], NORM_MIN ** 2, None, ALU.max).then_inc(s_["ssq"], 1)

            def apply_norms(s, pair, par):
                dve.wait_ge(s_["rep_mm"], count(s, 2, pair))
                dve.wait_ge(s_["summed"], 2 * count(s, 4, 2 * pair + 1))
                if live(s - 2):
                    dve.wait_ge(s_["p_mm"], count(s - 2, 8, 4 * pair + 3))
                if pair == 1 or live(s - 1):
                    dve.wait_ge(s_["moved"][1 - pair], count(s if pair == 1 else s - 1, 8, 7))
                for side in range(2):
                    u = g["unit"][2 * pair + side]
                    rn = bank_7[:, side * T:(side + 1) * T]
                    nc.vector.tensor_tensor(g["heads"][par][:, side, 2 * pair:2 * pair + 2, :],
                                            u[:, 0, :].unsqueeze(1).broadcast_to([128, 2, T]),
                                            rn.unsqueeze(1).broadcast_to([128, 2, T]), ALU.mult).then_inc(s_["in_place"], 1)
                    nc.vector.tensor_tensor(g["half_2"][side][:], u[:, 1, :], rn, ALU.mult).then_inc(s_["normed"], 1)

            def normalize(s, c, par):
                dve.wait_ge(s_["inv_den"], count(s, 4, c))
                if c == 0 and live(s - 2):
                    dve.wait_ge(s_["out_mm"], count(s - 2, 2, 1))
                nc.vector.tensor_tensor(g["oT"][par][:, c, :], bank_o[:, 0:T], g["inv_den"][:], ALU.mult).then_inc(s_["oT"], 1)

            def add_and_stats(s):
                dve.wait_ge(s_["out_mm"], count(s, 2, 1))
                nc.vector.tensor_tensor(z[:, rows(s), :], z[:, rows(s), :],
                                        bank_m[:, 0:T].rearrange("p (t d) -> p t d", d=D), ALU.add).then_inc(s_["z_set"], 1)
                dve.wait_ge(s_["z_set"], count(s, 1))
                dve.sem_inc(s_["dve_held"], 1)
                for i in range(TILES):
                    for half in range(2):
                        nc.vector.bn_stats(m["half_stats"][:, half, s * TILES + i, :],
                                           z[:, s * TILES + i, half * 64:half * 64 + 64]).then_inc(s_["half_stats"], 1)

            def period(p, par):
                for k in range(8):
                    if k == 1 and live(p - 1):
                        set_max(p - 1, 1 - par)
                    if k == 5 and live(p + 1):
                        clip_squares(p + 1)
                    if k == 6 and live(p + 1):
                        apply_norms(p + 1, 0, 1 - par)
                    if k in (1, 3) and live(p - 2):
                        normalize(p - 2, 2 + k // 2, par)
                    if k in (5, 7) and live(p - 1):
                        normalize(p - 1, k // 2 - 2, 1 - par)
                    if k == 1 and live(p):
                        apply_norms(p, 1, par)
                    if live(p):
                        row_max(p, k, par)
                    if k in (0, 2, 4) and live(p + 1):
                        rotate(p + 1, k // 2 + 1)
                    if k == 6 and live(p + 2):
                        rotate(p + 2, 0)
                    if k == 7 and live(p):
                        cut_max(p, par)
                    if k == 7 and live(p - 2):
                        add_and_stats(p - 2)

            periods(dve, period)

        @block.scalar
        def _(act):
            nc.scalar.preload_act_table_set("natural_log_exp_and_others")
            act.wait_ge(s_["w_in"], 64 * (layer + 1))
            for name in ("w_qk", "w_v"):
                nc.scalar.activation(g[name + "_hi"][:], g[name], ACT.Copy).then_inc(s_["w_hi"], 1)

            def exp_head(s, h):
                act.wait_ge(s_["p_mm"], count(s, 8, h))
                if h % 2 == 0 and (h >= 4 or live(s - 1)):
                    act.wait_ge(s_["o_mm"], count(s, 4, h // 2 - 2))
                nc.scalar.activation(g["probs"][:, h % 4, :], bank_p[h % 2][:, 0:320], ACT.Exp).then_inc(s_["p"], 1)

            def square(s, u):
                act.wait_ge(s_["qk_mm"], count(s, 4, u))
                if live(s - 1):
                    act.wait_ge(s_["ssq_mm"], count(s - 1, 1))
                elif u == 0:
                    act.wait_ge(s_["w_lo"], 2 * (layer + 1))
                nc.scalar.activation(g["sq"][u], bank_6[:].rearrange("p (a t) -> p a t", a=2), ACT.Square).then_inc(s_["squares"], 1)

            def move_halves(s, pair, side, par):
                act.wait_ge(s_["normed"], count(s, 4, 2 * pair + side))
                act.wait_ge(s_["in_place"], count(s, 4, 2 * pair + side))
                for b in range(4):
                    to = 32 * (b ^ 1)
                    nc.scalar.activation(g["heads"][par][to:to + 32, side, 2 * pair + b % 2, :],
                                         g["half_2"][side][32 * b:32 * b + 32, :], ACT.Copy).then_inc(s_["moved"][pair], 1)

            def invert_norms(s):
                act.wait_ge(s_["ssq"], count(s, 1))
                if live(s - 1):
                    act.wait_ge(s_["rnorm"], count(s - 1, 1))
                nc.scalar.activation(g["log_ssq"][:], g["ssq"][:], ACT.Ln, scale=NORM_SHIFT ** 2).then_inc(s_["log_norm"], 1)
                act.wait_ge(s_["log_norm"], count(s, 1))
                if live(s - 1):
                    act.wait_ge(s_["rn_lo"], count(s - 1, 1))
                nc.scalar.activation(g["rn"][:], g["log_ssq"][:], ACT.Exp, scale=-0.5).then_inc(s_["rnorm"], 1)
                act.wait_ge(s_["rnorm"], count(s, 1))
                if live(s - 1):
                    act.wait_ge(s_["rep_mm"], count(s - 1, 2, 1))
                nc.scalar.activation(g["rn_hi"][:], g["rn"][:], ACT.Copy).then_inc(s_["rn_hi"], 1)

            def invert_den(s, c):
                act.wait_ge(s_["o_mm"], count(s, 4, c))
                if c > 0 or live(s - 1):
                    act.wait_ge(s_["inv_den"], count(s, 4, c - 1))
                nc.scalar.activation(g["log_den"][:], bank_o[:, T:2 * T], ACT.Ln).then_inc(s_["log_den"], 1)
                act.wait_ge(s_["log_den"], count(s, 4, c))
                if c > 0 or live(s - 1):
                    act.wait_ge(s_["oT"], count(s, 4, c - 1))
                nc.scalar.activation(g["inv_den"][:], g["log_den"][:], ACT.Exp, scale=-1.0).then_inc(s_["inv_den"], 1)

            def set_hT(s, par):
                act.wait_ge(s_["hT_mm"], count(s, 1))
                if live(s - 1):
                    act.wait_ge(s_["hT_lo"], count(s - 1, 1))
                nc.scalar.activation(g["hT"][0:64, :], bank_m[0:64, 0:T], ACT.Copy).then_inc(s_["hT_psum"], 1)
                nc.scalar.activation(g["hT"][64:128, 1:T], bank_m[64:128, 0:T - 1], ACT.Copy).then_inc(s_["hT_psum"], 1)
                act.wait_ge(s_["hT_psum"], count(s, 2, 1))
                if live(s - 2):
                    act.wait_ge(s_["v_mm"], count(s - 2, 2, 1))
                nc.scalar.activation(g["hT_hi"][par][:], g["hT"][:], ACT.Copy).then_inc(s_["hT_hi"], 1)

            def set_v(s, i, par):
                act.wait_ge(s_["v_mm"], count(s, 2, i))
                if live(s - 2):
                    act.wait_ge(s_["o_mm"], count(s - 2, 4, 3))
                nc.scalar.activation(g["v"][par][:, i, :], bank_7[:], ACT.Copy).then_inc(s_["v"], 1)

            def period(p, par):
                for k in range(8):
                    s, h = e_head(p, k)
                    if k == 4 and live(p + 2):
                        set_hT(p + 2, par)
                    if k == 3 and live(p):
                        move_halves(p, 1, 1, par)
                    if k == 7 and live(p + 1):
                        move_halves(p + 1, 0, 1, 1 - par)
                    if k == 5 and live(p + 1):
                        invert_norms(p + 1)
                    if live(s):
                        exp_head(s, h)
                    if k == 2 and live(p):
                        move_halves(p, 1, 0, par)
                    if k in (0, 2) and live(p - 2):
                        invert_den(p - 2, 2 + k // 2)
                    if k in (4, 6) and live(p - 1):
                        invert_den(p - 1, k // 2 - 2)
                    if k == 6 and live(p + 1):
                        move_halves(p + 1, 0, 0, 1 - par)
                    if k in (1, 3) and live(p + 1):
                        square(p + 1, 2 + k // 2)
                    if k in (2, 3) and live(p):
                        set_v(p, k - 2, par)
                    if k in (5, 7) and live(p + 2):
                        square(p + 2, k // 2 - 2)

            periods(act, period)


def window_buffers(nc, ctx):
    def sb(name, shape, dt=F32):
        return ctx.enter_context(nc.sbuf_tensor("b_" + name, shape, dt))

    g = {name: sb(name, shape) for name, shape in dict(
        sq_all=[128, 4 * 2 * T], w_o=[128, 4 * D], scales=[128, 4],
        rope=[128, 2, 2, T], tab_c=[128, 2, 2, T], tab_s=[128, 2, 2, T],
        head_sum=[128, 32], ones=[128, 64],
        z_in=[128, TILES, D], ssq=[128, T], log_ssq=[128, T], rn=[128, T],
        probs=[128, 4, 320], log_den=[128, T], inv_den=[128, T], hT=[128, T],
    ).items()}
    for name, shape, n in (("oT", [128, 4, T], 2), ("rot_c", [128, 2, T], 2), ("rot_s", [128, 2, T], 2), ("half_2", [128, T], 2), ("unit", [128, 2, T], 4),
                           ("heads", [128, 2, 4, T], 2), ("v", [128, TILES, HB * DB], 2),
                           ("neg_max", [128, 2, HB], 2), ("rest", [128, 2, HB], 2)):
        g[name] = [sb(f"{name}{i}", shape) for i in range(n)]
    sq = g["sq_all"]
    g["sq"] = [sq[:, u * 2 * T:(u + 1) * 2 * T].rearrange("p (a t) -> p a t", a=2) for u in range(4)]
    g["w_qk"], g["w_v"], g["head_rep"] = sq[:, 0:8 * 128], sq[:, 8 * 128:8 * 128 + HB * DB], sq[:, 0:4 * 128]
    for name, width in (("w_qk", 8 * 128), ("w_v", HB * DB), ("rn", T)):
        for part in ("_hi", "_lo"):
            g[name + part] = sb(name + part, [128, width], F32R)
    for part in ("hT_hi", "hT_lo"):
        g[part] = [sb(f"{part}{i}", [128, T], F32R) for i in range(2)]
    g["head_rep_r"] = sb("head_rep_r", [128, 4 * 128], F32R)
    g["mask_q"] = sb("mask_q", [128, 320], BF16)
    g["mask_k"] = sb("mask_k", [128, 320], BF16)
    g["head_row"] = sb("head_row", [3 * HB, HB, 128], BF16)
    g["parts"] = sb("parts", [128, 2, 3 * HB], BF16)
    g["neg_maxT"] = [sb(f"neg_maxT{i}", [3 * HB, T], BF16) for i in range(2)]
    names = """w_in in_place normed moved0 moved1 p_mm rot summed hT_mm z_in z_set ssq hT_psum hT_hi hT_lo rn_hi rn_lo w_hi w_lo v v_mm qk_mm squares ssq_mm mT rnorm rep_mm
        max s_mm p oT o_mm cut mT_mm out_mm tables log_norm inv_den log_den half_stats pe_held dve_held pool_held sp_held""".split()
    g["sems"] = {name: ctx.enter_context(nc.semaphore("b_" + name)) for name in names}
    g["sems"]["moved"] = [g["sems"]["moved0"], g["sems"]["moved1"]]
    return g


def mlp_stage(nc, t, m, banks, w, layer, out):
    z, xa, ident = m["z"], m["xa"], m["ident"]
    g = w
    s_ = w["sems"]
    N = SEQS * TILES
    stats, mv, rb, rb_next = m["half_stats"], g["mv"], g["rb"], g["rb_next"]

    def count(seq, per_seq, unit=0):
        return (layer * SEQS + seq) * per_seq + unit + 1

    def rows(seq):
        return bass.ds(seq * TILES, TILES) if not isinstance(seq, int) else slice(seq * TILES, seq * TILES + TILES)

    def by_tile(a):
        return a.rearrange("p (s i) -> p i s", i=TILES)

    with nc.Block() as block:
        @block.sync
        def _(sp):
            for name in ("w_1", "w_2", "b_1", "norm"):
                sp.dma_start(g[name][:], t["c_" + name][bass.ds(layer, 1)].rearrange("l p n -> p (l n)")).then_inc(s_["w_in"], 16)
            sp.dma_start(g["b_2"][:], t["L0_ffn_b2"][bass.ds(layer, 1)].broadcast_to([128, D])).then_inc(s_["w_in"], 16)
            sp.wait_ge(s_["zero_stats"], layer + 1)
            sp.dma_start(g["moved"][1:128, :, :], stats[0:127, 1, :, :]).then_inc(s_["stats_in"], 16)
            odd, even = slice(1, N, 2), slice(0, N, 2)
            sp.dma_start(g["moved"][0:1, odd, :], stats[127:128, 1, even, :]).then_inc(s_["stats_in"], 16)
            sp.wait_ge(s_["rb"], 2 * (layer + 1))
            sp.dma_start(rb_next[0:127], rb[1:128]).then_inc(s_["next_in"], 16)
            sp.dma_start(rb_next[127:128, :, 0, :], rb[0:1, :, 1, :]).then_inc(s_["next_in"], 16)
            sp.dma_start(rb_next[127:128, 1, 1, :], rb[0:1, 1, 0, :]).then_inc(s_["next_in"], 16)
            sp.dma_start(rb_next[127:128, 0, 1, :], g["zeros"][0:1, 0:SEQS]).then_inc(s_["next_in"], 16)
            sp.wait_ge(s_["next_in"], 64 * (layer + 1))
            sp.sem_inc(s_["sp_held"], 1)
            sp.wait_ge(s_["w_in"], 80 * (layer + 1))
            sp.sem_inc(s_["sp_held"], 1)

        @block.vector
        def _(dve):
            nc.vector.bn_stats(g["zero_stats"][:], g["zeros"][0:1, 0:64]).then_inc(s_["zero1"], 1)
            dve.wait_ge(s_["zero1"], layer + 1)
            nc.vector.tensor_copy(g["moved"][0:1, 0:N:2, :], g["zero_stats"][:].unsqueeze(1).broadcast_to([1, N // 2, 6])
                                  ).then_inc(s_["zero_stats"], 1)
            dve.wait_ge(s_["zero_stats"], layer + 1)
            dve.wait_ge(s_["stats_in"], 32 * (layer + 1))
            nc.vector.tensor_copy(stats[:, 1, :, :], g["moved"][:]).then_inc(s_["stats_set"], 1)
            dve.wait_ge(s_["stats_set"], layer + 1)
            dve.sem_inc(s_["held"], 1)
            for n in range(N):
                nc.vector.bn_aggr(mv[:, n, :], stats[:, :, n, :]).then_inc(s_["mv"], 1)
            dve.wait_ge(s_["rb_r"], layer + 1)
            nc.vector.scalar_tensor_tensor(out=rb[:, 1], in0=by_tile(mv[:, :, 0]), scalar=-1.0, in1=rb[:, 0], op0=ALU.mult,
                                           op1=ALU.mult).then_inc(s_["rb"], 2)

        @block.scalar
        def _(act):
            nc.scalar.preload_act_table_set("natural_log_exp_and_others")
            act.wait_ge(s_["mv"], N * (layer + 1))
            nc.scalar.activation(g["log_var"][:], by_tile(mv[:, :, 1]), ACT.Ln, bias=m["eps"][:, 0:1]).then_inc(s_["log_var"], 1)
            act.wait_ge(s_["log_var"], layer + 1)
            nc.scalar.activation(rb[:, 0], g["log_var"][:], ACT.Exp, scale=-0.5).then_inc(s_["rb_r"], 1)

    def periods(eng, period):
        for p in range(-2, 4):
            period(p, p % 2)
        with eng.Fori(2, (SEQS - 2) // 2) as i:
            for par in range(2):
                period(i * 2 + par, par)
        for p in range(SEQS - 2, SEQS + 2):
            period(p, p % 2)

    bank_g, bank_a, bank_2 = banks[0:2], banks[2:4], banks[4:6]
    bank_t, bank_o = banks[6], banks[7]

    with nc.Block() as block:
        @block.gpsimd
        def _(pool):
            def period(p, par):
                if live(p + 1):
                    pool.wait_ge(s_["xn"], count(p + 1, 4, 3))
                    nc.gpsimd.tensor_tensor(z[:, rows(p + 1), :], z[:, rows(p + 1), :],
                                            g["b_2"][:].unsqueeze(1).broadcast_to([128, TILES, D]), ALU.add).then_inc(s_["zb"], 1)
                if live(p - 2):
                    pool.wait_ge(s_["z_set"], count(p - 2, 1))
                    if live(p - 4):
                        pool.wait_ge(s_["stored"][par], landed(layer * SEQS + p - 4, par))
                    nc.gpsimd.tensor_tensor(g["res"][par][:], z[:, rows(p - 2), :], xa[:, rows(p - 2), :],
                                            ALU.add).then_inc(s_["res"], 1)

            periods(pool, period)

        @block.sync
        def _(sp):
            def period(p, par):
                if live(p - 2):
                    sp.wait_ge(s_["res"], count(p - 2, 1))
                    if live(p - 4):
                        sp.wait_ge(s_["stored"][par], landed(layer * SEQS + p - 4, par))
                    sp.sem_inc(s_["sp_held"], 1)
                    dst = out[bass.ds(p - 2, 1)] if not isinstance(p, int) else out[p - 2:p - 1]
                    sp.dma_start(dst.rearrange("n (t p) d -> p (n t) d", p=128), g["res"][par][:]
                                 ).then_inc(s_["stored"][par], 16)

            periods(sp, period)
            for par in range(2):
                sp.wait_ge(s_["stored"][par], landed(layer * SEQS + SEQS - 2 + par, par))
                sp.sem_inc(s_["sp_held"], 1)

        @block.tensor
        def _(pe):
            def period(p, par):
                if live(p + 1):
                    pe.wait_ge(s_["xn"], count(p + 1, 4, 3))
                    if live(p):
                        pe.wait_ge(s_["hT"], count(p, 3, 2))
                    for i in range(TILES):
                        last = nc.tensor.transpose(bank_t[:, i * 128:(i + 1) * 128], g["xn"][:, i, :], ident[:])
                    last.then_inc(s_["hT_mm"], 1)
                if live(p):
                    pe.wait_ge(s_["hT"], count(p, 3, 2))
                    if live(p - 2):
                        pe.wait_ge(s_["hid"], count(p - 2, 3, 2))
                    for bank, chunks in ((bank_g[par], (3, 4)), (bank_2[par], (5, 2)), (bank_a[par], (0, 1))):
                        for i, c in enumerate(chunks):
                            last = nc.tensor.matmul(bank[0:HC, i * T:(i + 1) * T], g["w_1"][:, c * HC:(c + 1) * HC],
                                                    g["hT"][par][:], start=True, stop=True)
                        last.then_inc(s_["up_mm"], 1)
                if live(p - 1):
                    pe.wait_ge(s_["hid"], count(p - 1, 3, 2))
                    if live(p - 2):
                        pe.wait_ge(s_["z_set"], count(p - 2, 1))
                    for i in range(TILES):
                        for c in range(3):
                            last = nc.tensor.matmul(bank_o[:, i * D:(i + 1) * D], g["hid"][1 - par][:, c, i * 128:(i + 1) * 128],
                                                    g["w_2"][0:HC, c * D:(c + 1) * D], start=(c == 0), stop=(c == 2))
                    last.then_inc(s_["down_mm"], 1)

            periods(pe, period)

        @block.scalar
        def _(act):
            def set_hT(s, par):
                act.wait_ge(s_["hT_mm"], count(s, 1))
                if live(s - 2):
                    act.wait_ge(s_["up_mm"], count(s - 2, 3, 2))
                for r, dst, src in ((slice(0, 64), slice(0, T), slice(0, T)), (slice(64, 128), slice(1, T), slice(0, T - 1)),
                                    (slice(64, 128), slice(0, 1), slice(T - 1, T))):
                    nc.scalar.activation(g["hT"][par][r, dst], bank_t[r, src], ACT.Identity, scale=g["norm"][r, 0:1],
                                         bias=g["norm"][r, 1:2]).then_inc(s_["hT"], 1)

            def gelu(s, par):
                for c in range(3):
                    act.wait_ge(s_["up_mm"], count(s, 3, c // 2))
                    if live(s - 2):
                        act.wait_ge(s_["hid"], count(s - 2, 3, c))
                    src = bank_2[par][0:HC, 0:T] if c == 2 else bank_g[par][0:HC, c * T:(c + 1) * T]
                    nc.scalar.activation(g["gate"][par][:, c, :], src, ACT.Gelu, bias=g["b_1"][0:HC, 3 + c:4 + c]
                                         ).then_inc(s_["gate"], 1)

            def period(p, par):
                if live(p + 1):
                    set_hT(p + 1, 1 - par)
                if live(p):
                    gelu(p, par)

            periods(act, period)

        @block.vector
        def _(dve):
            def period(p, par):
                if live(p - 2):
                    dve.wait_ge(s_["down_mm"], count(p - 2, 1))
                    dve.wait_ge(s_["zb"], count(p - 2, 1))
                    nc.vector.tensor_tensor(z[:, rows(p - 2), :], z[:, rows(p - 2), :],
                                            bank_o[:, 0:T].rearrange("p (t d) -> p t d", d=D), ALU.add).then_inc(s_["z_set"], 1)
                if live(p - 1):
                    q = 1 - par
                    for c in range(3):
                        dve.wait_ge(s_["gate"], count(p - 1, 3, 2))
                        dve.wait_ge(s_["up_mm"], count(p - 1, 3, 2))
                        if live(p - 3):
                            dve.wait_ge(s_["down_mm"], count(p - 3, 1))
                        src = bank_2[q][0:HC, T:2 * T] if c == 2 else bank_a[q][0:HC, c * T:(c + 1) * T]
                        nc.vector.scalar_tensor_tensor(out=g["hid"][q][:, c, :], in0=src, scalar=g["b_1"][0:HC, c:c + 1],
                                                       in1=g["gate"][q][:, c, :], op0=ALU.add, op1=ALU.mult
                                                       ).then_inc(s_["hid"], 1)
                if live(p + 2):
                    if live(p + 1):
                        dve.wait_ge(s_["hT_mm"], count(p + 1, 1))
                    for i in range(TILES):
                        n = (p + 2) * TILES + i
                        for half, v in ((0, rb), (1, rb_next)):
                            f = slice(64 * half, 64 * half + 64)
                            nc.vector.tensor_scalar(g["xn"][:, i, f], z[:, n, f], v[:, 0, i, bass.ds(p + 2, 1)],
                                                    v[:, 1, i, bass.ds(p + 2, 1)], ALU.mult, ALU.add).then_inc(s_["xn"], 1)

            periods(dve, period)


def mlp_buffers(nc, ctx):
    def sb(name, shape, dt=F32):
        return ctx.enter_context(nc.sbuf_tensor("c_" + name, shape, dt))

    N = SEQS * TILES
    g = {name: sb(name, shape) for name, shape in dict(
        w_1=[128, 6 * HC], w_2=[128, 3 * D], b_1=[128, 6], norm=[128, 2], b_2=[128, D],
        moved=[128, N, 6], zeros=[1, 64], zero_stats=[1, 6], mv=[128, N, 2], log_var=[128, TILES, SEQS],
        rb=[128, 2, TILES, SEQS], rb_next=[128, 2, TILES, SEQS], xn=[128, TILES, D],
    ).items()}
    for name, shape in (("hT", [128, T]), ("gate", [HC, 3, T]), ("hid", [HC, 3, T]), ("res", [128, TILES, D])):
        g[name] = [sb(f"{name}{i}", shape) for i in range(2)]
    names = """w_in zero1 zero_stats stats_in stats_set mv rb rb_r log_var next_in sp_held held xn zb z_set stored0 stored1 res hT hT_mm
        hid up_mm down_mm gate""".split()
    g["sems"] = {name: ctx.enter_context(nc.semaphore("c_" + name)) for name in names}
    g["sems"]["stored"] = [g["sems"]["stored0"], g["sems"]["stored1"]]
    return g


def layouts(x):
    bf = np.dtype("bfloat16")
    f = np.float32
    c = {}
    c["ident"] = np.eye(128, dtype=f)
    c["identb"] = np.eye(128, dtype=f).astype(bf)
    mr, k_ones = np.zeros((3 * HA, CHUNKS, 128), f), np.zeros((128, 1), f)
    for part in range(3):
        for h in range(HA):
            mr[part * HA + h, h // 4, 32 * (h % 4) + 3 * DA + part] = 1
            k_ones[32 * (h % 4) + 3 * DA + part] = 1
    c["a_max_rows"], c["a_k_ones"] = mr.astype(bf), k_ones
    wT = np.ascontiguousarray(x["L0_attn_W_qkv"].T)
    swap = np.arange(128) ^ 1
    c["a_w_qk"] = np.stack([wT[:, 0:128], wT[:, 128:256], wT[:, 0:128][:, swap], wT[:, 128:256][:, swap]], 1)
    c["a_w_v"] = wT[:, 256:384]
    woT = x["L0_attn_W_out"].T
    wo = np.zeros((128, CHUNKS, 128), f)
    for h in range(HA):
        wo[32 * (h % 4):32 * (h % 4) + DA, h // 4, :] = woT[DA * h:DA * h + DA, :]
    c["a_w_out"] = wo
    freqs = (1.0 / np.float32(10000.0) ** (np.arange(0, DA, 2, dtype=f) / DA)).astype(f)
    ang = np.outer(np.arange(T, dtype=f), freqs).astype(f)
    cos, sin = np.cos(ang).astype(f), np.sin(ang).astype(f)
    pair = (np.arange(128) % DA) // 2
    rc = cos.T[pair]
    rs = sin.T[pair] * np.where(np.arange(128) % 2 == 0, -1, 1).astype(f)[:, None]
    c["a_rope_c"] = np.stack([rc, rc], 1)
    c["a_rope_s"] = np.stack([rs, rs], 1)
    tri = np.where(np.arange(128)[None, :] > np.arange(128)[:, None], MASKED, 0.0)
    c["a_mask_q"] = np.stack([tri, tri], 1).astype(bf)
    sel = np.zeros((128, 2, 2, CHUNKS, 128), f)
    for side, order in enumerate(((0, 0, 1), (0, 1, 0))):
        for h in range(HA):
            for slot, part in enumerate(order):
                for d in range(DA):
                    sel[DA * h + d, side, part, h // 4, 32 * (h % 4) + DA * slot + d] = 1
    c["a_sel"] = sel.reshape(128, -1)
    wqkv = x["L0_ffn_wqkv"]
    inner = HB * DB
    cols = [side * inner + (4 * g + j) * DB + half * 32 + d
            for g in range(2) for side in range(2) for half in range(2) for j in (0, 2, 1, 3) for d in range(32)]
    c["b_w_qk"] = wqkv[:, :, cols]
    c["b_w_v"] = wqkv[:, :, 2 * inner:]
    c["b_w_o"] = x["L0_ffn_wo"].reshape(DEPTH, 4, 128, D).transpose(0, 2, 1, 3).reshape(DEPTH, 128, 4 * D)
    c["b_scales"] = np.stack([np.tile(x[name][:, half * 32:half * 32 + 32], (1, 4))
                              for name in ("L0_ffn_q_scale", "L0_ffn_k_scale") for half in range(2)], 2)
    half_idx = np.arange(0, DB, 2, dtype=f)
    inv_freq = (1.0 / np.float32(10000.0) ** (half_idx / DB)).astype(f)
    pos = np.arange(T, dtype=f)
    ang = (pos[:, None] * inv_freq[None, :]).astype(f)
    base = ((half_idx + np.float32(0.4 * DB)) / np.float32(1.4 * DB)).astype(f)
    power = ((pos - T // 2) / np.float32(WINDOW // 2)).astype(f)
    xpos = (base[None, :] ** power[:, None]).astype(f)
    cos, sin = np.cos(ang).astype(f), np.sin(ang).astype(f)
    tab = [[NORM_SHIFT * QK_SCALE * cos * xpos, NORM_SHIFT * QK_SCALE * sin * xpos],
           [NORM_SHIFT * cos / xpos, NORM_SHIFT * sin / xpos]]
    c["b_rope"] = np.stack([np.stack([np.tile(a.T, (4, 1)) for a in side], 1) for side in tab], 1).astype(f)
    head = np.arange(128) // 32
    hs = np.zeros((128, 32), f)
    hs[np.arange(128), head] = 1
    c["b_head_sum"] = hs
    rep = np.zeros((128, 4, 128), f)
    for u in range(4):
        rep[32 * u + head, u, np.arange(128)] = 1
    c["b_head_rep"] = rep.reshape(128, -1)
    p, n = np.arange(128)[:, None], np.arange(320)[None, :]
    q, k = np.where(n < 128, p, 128 + p), np.where(n < 128, n, n - 64)
    c["b_mask_q"] = np.where((q >= k) & (q <= k + WINDOW), 0.0, MASKED).astype(bf)
    q, k = np.where(n < 192, n, n - 64), np.where(n < 192, p, 128 + p)
    c["b_mask_k"] = np.where((q >= k) & (q <= k + WINDOW), 0.0, MASKED).astype(bf)
    hr = np.zeros((3 * HB, HB, 128), f)
    for part in range(3):
        for h in range(HB):
            hr[part * HB + h, h, :] = 1
    c["b_head_row"] = hr.astype(bf)
    def chunked(a, axis):
        pad = [(0, 0)] * a.ndim
        pad[axis] = (0, 3 * HC - HIDDEN)
        return np.pad(a, pad)
    w1, b1, w2 = x["L0_ffn_w1"], x["L0_ffn_b1"], x["L0_ffn_w2"]
    c["c_w_1"] = np.concatenate([chunked(w1[:, :, :HIDDEN], 2), chunked(w1[:, :, HIDDEN:], 2)], 2)
    b = np.concatenate([chunked(b1[:, :HIDDEN], 1), chunked(b1[:, HIDDEN:], 1)], 1).reshape(DEPTH, 6, HC)
    c["c_b_1"] = np.pad(b.transpose(0, 2, 1), ((0, 0), (0, 128 - HC), (0, 0)))
    c["c_w_2"] = np.pad(chunked(w2, 1).reshape(DEPTH, 3, HC, D).transpose(0, 2, 1, 3),
                        ((0, 0), (0, 128 - HC), (0, 0), (0, 0))).reshape(DEPTH, 128, 3 * D)
    c["c_norm"] = np.stack([x["L0_ffn_ln_g"], x["L0_ffn_ln_b"]], 2)
    c["L0_ffn_b2"] = x["L0_ffn_b2"]
    return c


def kernel(**inputs):
    import concourse.bacc as bacc
    from concourse.bass_utils import run_bass_kernel_spmd

    nc = bacc.Bacc("TRN2", target_bir_lowering=False, num_devices=1)
    x = {k: np.ascontiguousarray(v) for k, v in inputs.items()}
    arrays = {"L0_attn_x": x["L0_attn_x"], **layouts(x)}
    arrays = {k + "_dram": np.ascontiguousarray(v) for k, v in arrays.items()}
    t = {k[:-5]: nc.dram_tensor(k, v.shape, mybir.dt.from_np(v.dtype), kind="ExternalInput").ap() for k, v in arrays.items()}
    out = nc.dram_tensor("out", (SEQS, T, D), F32, kind="ExternalOutput").ap()
    build(nc, t, out)
    r = run_bass_kernel_spmd(nc, [arrays], core_ids=[0])
    return r.results[0]["out"]
```

```python
import numpy as np

from contextlib import ExitStack

import concourse.bass as bass
from concourse import mybir

F32 = mybir.dt.float32
F32R = mybir.dt.float32r
BF16 = mybir.dt.bfloat16
ALU = mybir.AluOpType
ACT = mybir.ActivationFunctionType
AX = mybir.AxisListType

SEQS, T, D = 32, 256, 128
TILES = T // 128
EPS = 1e-5
MASKED = -1e30

HA, DA = 16, 8
CHUNKS = HA // 4
SCALE_A = float(np.float32(1.0) / np.sqrt(np.float32(DA)))

HB, DB, WINDOW = 8, 64, 64
NORM_MIN, NORM_SHIFT = 1e-12, 256.0
QK_SCALE = 8.0

HIDDEN = int(D * 4 * 2 / 3)
HC = 114

DEPTH = 2


def live(seq):
    return not isinstance(seq, int) or 0 <= seq < SEQS


def count(seq, per_seq, unit=0):
    return seq * per_seq + unit + 1


def landed(seq, parity):
    return seq * 8 + (16 - 8 * parity)


def masked_max(nc, neg_max, scores, mask):
    return nc.vector.tensor_tensor_reduce(out=scores, in0=scores, in1=mask, scale=-1.0, scalar=-MASKED, op0=ALU.add,
                                          op1=ALU.min, accum_out=neg_max)


def build(nc, t, out):
    with ExitStack() as ctx:
        def sb(name, shape, dt=F32):
            return ctx.enter_context(nc.sbuf_tensor(name, shape, dt))

        banks = [ctx.enter_context(nc.psum_tensor(f"bank{i}", [128, 512], F32)) for i in range(8)]
        m = dict(
            xa=sb("xa", [128, SEQS * TILES, D]),
            z=sb("z", [128, SEQS * TILES, D]),
            ident=sb("ident", [128, 128]),
            identb=sb("identb", [128, 128], BF16),
            eps=sb("eps", [128, 1]),
        )
        attention_stage(nc, t, m, banks)
        m["half_stats"] = sb("half_stats", [128, 2, SEQS * TILES, 6])
        window = window_buffers(nc, ctx)
        mlp = mlp_buffers(nc, ctx, window)
        constants(nc, ctx, t, window, mlp)
        with nc.Fori(0, DEPTH) as layer:
            window_stage(nc, t, m, banks, window, layer)
            mlp_stage(nc, t, m, banks, mlp, layer, out)


def constants(nc, ctx, t, window, mlp):
    loaded = ctx.enter_context(nc.semaphore("const_loaded"))
    names = ("rope", "head_sum", "head_rep", "mask_q", "mask_k", "head_row")
    with nc.Block() as block:
        @block.sync
        def _(sp):
            for name in names:
                dst = window[name] if name == "head_rep" else window[name][:]
                sp.dma_start(dst, t["b_" + name]).then_inc(loaded, 16)
            sp.wait_ge(loaded, 16 * len(names))

        @block.vector
        def _(dve):
            nc.vector.memset(window["hT"][64:128, 0:1], 0.0)
            dve.wait_ge(loaded, 16 * len(names))
            nc.vector.tensor_copy(window["head_rep_r"][:], window["head_rep"])
            nc.vector.memset(mlp["zeros"][:], 0.0)


def attention_stage(nc, t, m, banks):
    xa, z, ident, identb, eps = (m[k] for k in ("xa", "z", "ident", "identb", "eps"))
    with ExitStack() as ctx:
        def sb(name, shape, dt=F32):
            return ctx.enter_context(nc.sbuf_tensor("a_" + name, shape, dt))

        def sem(name):
            return ctx.enter_context(nc.semaphore("a_" + name))

        w_qk = sb("w_qk", [128, 4, 128])
        w_v = sb("w_v", [128, 128])
        w_out = sb("w_out", [128, CHUNKS, 128])
        rope_c = sb("rope_c", [128, 2, T])
        rope_s = sb("rope_s", [128, 2, T])
        mask_q = sb("mask_q", [128, 3 * 128])
        max_rows = sb("max_rows", [3 * HA, CHUNKS, 128], BF16)
        k_ones = sb("k_ones", [128, 1])
        sel_raw = sb("sel_raw", [128, 16 * 128])
        sel = sb("sel", [128, 2, 2, CHUNKS, 128], F32R)
        ones = sb("ones", [128, 32])
        xn = sb("xn", [128, TILES, D])
        stats = sb("stats", [128, 2, 6])
        mean_var = sb("mean_var", [128, 2, 2])
        log_var = sb("log_var", [128, 2])
        rstd = sb("rstd", [128, 2])
        stats2 = sb("stats2", [128, 2, 6])
        mean_var2 = sb("mean_var2", [128, 2, 2])
        log_var2 = sb("log_var2", [128, 2])
        rstd2 = sb("rstd2", [128, 2])
        xT = [sb(f"xT{i}", [128, T]) for i in range(2)]
        rot_c = sb("rot_c", [128, 2, T])
        rot_s = sb("rot_s", [128, 2, T])
        qk = sb("qk", [128, 2, T])
        qk_hi = sb("qk_hi", [128, 2, T], F32R)
        qk_lo = sb("qk_lo", [128, 2, T], F32R)
        slots = [sb(f"slots{i}", [128, CHUNKS, 2, T], F32R) for i in range(2)]
        v = [sb(f"v{i}", [128, TILES, HA, 32]) for i in range(2)]
        neg_max = [sb(f"neg_max{i}", [128, 2, HA]) for i in range(2)]
        rest1 = sb("rest1", [128, 2, HA])
        rest2 = sb("rest2", [128, 2, HA])
        parts = sb("parts", [128, 2, 3 * HA], BF16)
        neg_maxT = [sb(f"neg_maxT{i}", [3 * HA, T], BF16) for i in range(2)]
        probs = sb("probs", [128, 8, 384])
        log_den = sb("log_den", [128, T])
        inv_den = sb("inv_den", [128, T])
        oT = sb("oT", [128, CHUNKS, T])
        bank_s, bank_p, bank_o, bank_m, bank_6, bank_7 = banks[0:2], banks[2:4], banks[4], banks[5], banks[6], banks[7]
        partsT = bank_m[:, 0:T // 2].bitcast(BF16)

        const_in = sem("const_in")
        x_in = [sem("x_in0"), sem("x_in1")]
        const_set = sem("const_set")
        sel_set = sem("sel_set")
        stats_set = sem("stats_set")
        mv_set = sem("mv_set")
        logv_set = sem("logv_set")
        rstd_set = sem("rstd_set")
        xn_centred, z_centred = sem("xn_centred"), sem("z_centred")
        xn_set = sem("xn_set")
        stats2_set = sem("stats2_set")
        mv2_set = sem("mv2_set")
        logv2_set = sem("logv2_set")
        rstd2_set = sem("rstd2_set")
        z_set = sem("z_set")
        xT_mm = sem("xT_mm")
        xT_set = sem("xT_set")
        qk_mm = sem("qk_mm")
        swap_mm = sem("swap_mm")
        v_mm = sem("v_mm")
        v_set = sem("v_set")
        rot_c_set = sem("rot_c_set")
        rot_s_set = sem("rot_s_set")
        qk_set = sem("qk_set")
        hi_set = sem("hi_set")
        lo_set = sem("lo_set")
        sel_mm = sem("sel_mm")
        slots_set = sem("slots_set")
        s_mm = sem("s_mm")
        max_set = sem("max_set")
        m_step = sem("m_step")
        mT_mm = sem("mT_mm")
        mT_set = sem("mT_set")
        p_mm = sem("p_mm")
        mx_mm = sem("mx_mm")
        mx_set = sem("mx_set")
        p_exp = sem("p_exp")
        p_set = sem("p_set")
        o_mm = sem("o_mm")
        logd_set = sem("logd_set")
        invd_set = sem("invd_set")
        oT_set = sem("oT_set")
        out_mm = sem("out_mm")
        xa_set = sem("xa_set")
        dve_held, pe_held, pool_held = sem("dve_held"), sem("pe_held"), sem("pool_held")

        block = ctx.enter_context(nc.Block())
        x_tiles = t["L0_attn_x"].rearrange("n (t p) d -> n p t d", p=128)
        N_CONST = 11
        LAG = 6

        def e_head(p, k):
            return (p - 1, k - LAG) if k >= LAG else (p - 2, 16 - LAG + k)

        def rows(seq):
            return bass.ds(seq * TILES, TILES) if not isinstance(seq, int) else slice(seq * TILES, seq * TILES + TILES)

        def tile(buf, seq, i):
            return buf[:, seq * TILES + i, :]

        def periods(eng, period):
            for p in range(-2, 4):
                period(p, p % 2)
            with eng.Fori(2, (SEQS - 2) // 2) as i:
                for par in range(2):
                    period(i * 2 + par, par)
            for p in range(SEQS - 2, SEQS + 2):
                period(p, p % 2)

        @block.sync
        def _(sp):
            for name, dst in (("ident", ident[:]), ("identb", identb[:])):
                sp.dma_start(dst, t[name]).then_inc(const_in, 16)
            for name, dst in (("w_qk", w_qk[:]), ("w_v", w_v[:]), ("w_out", w_out[:]), ("rope_c", rope_c[:]),
                              ("rope_s", rope_s[:]), ("mask_q", mask_q[:]), ("max_rows", max_rows[:]), ("k_ones", k_ones[:]),
                              ("sel", sel_raw[:])):
                sp.dma_start(dst, t["a_" + name]).then_inc(const_in, 16)
            for s in range(2):
                sp.dma_start(xa[:, rows(s), :], x_tiles[s]).then_inc(x_in[s], 16)
            with sp.Fori(1, SEQS // 2) as i:
                for par in range(2):
                    s = i * 2 + par
                    sp.wait_ge(x_in[par], landed(s - 2, par))
                    sp.dma_start(xa[:, rows(s), :], x_tiles[bass.ds(s, 1)].rearrange("n p t d -> p (n t) d")).then_inc(x_in[par], 16)

        @block.gpsimd
        def _(pool):
            nc.gpsimd.memset(v[0][:], 0.0).then_inc(const_set, 1)
            nc.gpsimd.memset(v[1][:], 0.0).then_inc(const_set, 1)
            nc.gpsimd.memset(ones[:], 1.0).then_inc(const_set, 1)
            nc.gpsimd.memset(eps[:], EPS).then_inc(const_set, 1)

            def mask(s, h):
                pool.wait_ge(p_exp, count(s, 16, h))
                pool.sem_inc(pool_held, 1)
                diag = probs[:, h % 8, :].rearrange("p (a n) -> p a n", n=128)[:, 0:3:2, :]
                nc.gpsimd.affine_select(out=diag, in_=diag, pattern=[[0, 2], [1, 128]], compare_op=ALU.is_ge, fill=0.0,
                                        base=0, channel_multiplier=-1).then_inc(p_set, 1)

            def norm_apply(s, dst, mv, rs, centred, dst_sem):
                wide = [128, TILES, D]
                pool.sem_inc(pool_held, 1)
                nc.gpsimd.tensor_tensor(dst, xa[:, rows(s), :], mv[:, :, 0:1].broadcast_to(wide), ALU.subtract).then_inc(centred, 1)
                pool.wait_ge(centred, count(s, 1))
                pool.sem_inc(pool_held, 1)
                nc.gpsimd.tensor_tensor(dst, dst, rs[:].unsqueeze(2).broadcast_to(wide), ALU.mult).then_inc(dst_sem, 1)

            def add_rotated(p):
                if live(p + 1):
                    pool.wait_ge(rot_c_set, count(p + 1, 1))
                    pool.wait_ge(rot_s_set, count(p + 1, 1))
                    if live(p):
                        pool.wait_ge(hi_set, count(p, 1))
                        pool.wait_ge(lo_set, count(p, 1))
                    nc.gpsimd.tensor_tensor(qk[:], rot_c[:], rot_s[:], ALU.add).then_inc(qk_set, 1)

            def low_part(p):
                if live(p + 1):
                    pool.wait_ge(hi_set, count(p + 1, 1))
                    pool.wait_ge(qk_set, count(p + 1, 1))
                    if live(p):
                        pool.wait_ge(sel_mm, count(p, 4, 3))
                    nc.gpsimd.tensor_tensor(qk_lo[:], qk[:], qk_hi[:].bitcast(F32), ALU.subtract).then_inc(lo_set, 1)

            def period(p, par):
                for k in range(16):
                    s, h = e_head(p, k)
                    if live(s):
                        mask(s, h)
                    if k == 15 and live(p - 2):
                        pool.wait_ge(rstd2_set, count(p - 2, 1))
                        norm_apply(p - 2, z[:, rows(p - 2), :], mean_var2, rstd2, z_centred, z_set)
                    if k == 11 and live(p + 2):
                        pool.wait_ge(rstd_set, count(p + 2, 1))
                        if live(p + 1):
                            pool.wait_ge(xT_mm, count(p + 1, 1))
                        norm_apply(p + 2, xn[:], mean_var, rstd, xn_centred, xn_set)
                    if k == 8:
                        add_rotated(p)
                    if k == 10:
                        low_part(p)

            periods(pool, period)

        @block.tensor
        def _(pe):
            pe.wait_ge(const_in, 16 * N_CONST)
            pe.wait_ge(const_set, 4)
            pe.wait_ge(sel_set, 1)

            def transpose_x(s):
                pe.wait_ge(xn_set, count(s, 1))
                if live(s - 2):
                    pe.wait_ge(v_set, count(s - 2, 1))
                elif live(s - 1):
                    pe.wait_ge(rot_s_set, count(s - 1, 1))
                for i in range(TILES):
                    last = nc.tensor.transpose(bank_7[:, i * 128:(i + 1) * 128], xn[:, i, :], ident[:])
                last.then_inc(xT_mm, 1)

            def project_qk(s, par):
                pe.wait_ge(xT_set, count(s, 1))
                if live(s - 1):
                    pe.wait_ge(slots_set, 2 * count(s - 1, 4, 2))
                for i in range(2):
                    last = nc.tensor.matmul(bank_6[:, i * T:(i + 1) * T], w_qk[:, i, :], xT[par][:], start=True, stop=True)
                last.then_inc(qk_mm, 1)

            def project_swapped(s, par):
                for i in range(2):
                    last = nc.tensor.matmul(bank_7[:, i * T:(i + 1) * T], w_qk[:, 2 + i, :], xT[par][:], start=True, stop=True)
                last.then_inc(swap_mm, 1)

            def project_v(s, par):
                if live(s + 1):
                    pe.wait_ge(rot_s_set, count(s + 1, 1))
                else:
                    pe.wait_ge(v_set, count(s - 1, 1))
                for i in range(TILES):
                    last = nc.tensor.matmul(bank_7[:, i * 128:(i + 1) * 128], xT[par][:, i * 128:(i + 1) * 128], w_v[:],
                                            start=True, stop=True)
                last.then_inc(v_mm, 1)

            def spread(s, c):
                pe.wait_ge(lo_set, count(s, 1))
                if c == 0:
                    pe.wait_ge(rot_c_set, count(s, 1))
                    if live(s - 1):
                        pe.wait_ge(slots_set, 2 * count(s - 1, 4, 3))
                else:
                    pe.wait_ge(slots_set, 2 * count(s, 4, c - 1))
                    if c == 3 and live(s + 1):
                        pe.wait_ge(rot_c_set, count(s + 1, 1))
                for i in range(2):
                    dst = bank_6[:, i * T:(i + 1) * T]
                    nc.tensor.matmul(dst, sel[:, i, 0, c, :], qk_hi[:, i, :], start=True, stop=False)
                    last = nc.tensor.matmul(dst, sel[:, i, 1, c, :], qk_lo[:, i, :], start=False, stop=True)
                last.then_inc(sel_mm, 1)

            def score(s, h, par):
                if h % 4 == 0:
                    pe.wait_ge(slots_set, 2 * count(s, 4, h // 4))
                if h >= 2 or live(s - 1):
                    pe.wait_ge(max_set, 2 * count(s, 16, h - 2))
                r = slice(32 * (h % 4), 32 * (h % 4) + 32)
                q, k, bank = slots[par][r, h // 4, 0, :], slots[par][r, h // 4, 1, :], bank_s[h % 2]
                nc.tensor.matmul(bank[:, 0:128], q[:, 0:128], k[:, 0:128], start=True, stop=False, skip_group_check=True)
                nc.tensor.matmul(bank[:, 128:384], q[:, 128:256], k[:, 0:256], start=False, stop=True,
                                 skip_group_check=True).then_inc(s_mm, 1)

            def score_t(s, h, par):
                if h % 8 == 0:
                    pe.wait_ge(mx_set, count(s, 2, h // 8))
                if h >= 2 or live(s - 1):
                    pe.wait_ge(p_exp, count(s, 16, h - 2))
                r = slice(32 * (h % 4), 32 * (h % 4) + 32)
                q, k, bank = slots[par][r, h // 4, 0, :], slots[par][r, h // 4, 1, :], bank_p[h % 2]
                nc.tensor.matmul(bank[:, 0:256], k[:, 0:128], q[:, 0:256], start=True, stop=False, skip_group_check=True)
                nc.tensor.matmul(bank[:, 256:384], k[:, 128:256], q[:, 128:256], start=False, stop=True,
                                 skip_group_check=True).then_inc(p_mm, 1)

            def place_max(s, pair, par):
                if pair == 0:
                    pe.wait_ge(mT_set, count(s, 1))
                else:
                    pe.wait_ge(mx_set, count(s, 2, 0))
                for i in range(2):
                    last = nc.tensor.matmul(bank_m[:, i * T:(i + 1) * T], max_rows[:, 2 * pair + i, :], neg_maxT[par][:],
                                            start=True, stop=True)
                last.then_inc(mx_mm, 1)

            def weigh(s, c, par):
                pe.wait_ge(p_set, count(s, 16, 4 * c + 3))
                if c == 0:
                    pe.wait_ge(v_set, count(s, 1))
                if c > 0 or live(s - 1):
                    pe.wait_ge(oT_set, count(s, 4, c - 1))
                for half in range(2):
                    for kt in range(2):
                        for j in range(4):
                            h = 4 * c + j
                            lhs = v[par][:, kt, h, :] if half == 0 else ones[:]
                            dst = bank_o[32 * j:32 * j + 32, half * T + kt * 128:half * T + 256]
                            src = probs[:, h % 8, 0:256] if kt == 0 else probs[:, h % 8, 256:384]
                            last = nc.tensor.matmul(dst, lhs, src, start=(kt == 0), stop=(kt == 1), skip_group_check=True)
                last.then_inc(o_mm, 1)

            def transpose_max(s):
                pe.wait_ge(m_step, count(s, 5, 4))
                if live(s - 2):
                    pe.wait_ge(xa_set, count(s - 2, 1))
                elif live(s - 1):
                    pe.wait_ge(mx_set, count(s - 1, 2, 1))
                pe.sem_inc(pe_held, 1)
                for i in range(2):
                    last = nc.tensor.transpose(partsT[0:3 * HA, i * 128:(i + 1) * 128], parts[:, i, :], identb[:])
                last.then_inc(mT_mm, 1)

            def project_out(s, i):
                pe.wait_ge(oT_set, count(s, 4, 3))
                if i == 1:
                    pass
                elif live(s + 1):
                    pe.wait_ge(mx_set, count(s + 1, 2, 1))
                elif live(s - 1):
                    pe.wait_ge(xa_set, count(s - 1, 1))
                for c in range(CHUNKS):
                    last = nc.tensor.matmul(bank_m[:, i * 128:(i + 1) * 128], oT[:, c, i * 128:(i + 1) * 128],
                                            w_out[:, c, :], start=(c == 0), stop=(c == CHUNKS - 1))
                last.then_inc(out_mm, 1)

            def period(p, par):
                for k in range(16):
                    if live(p):
                        score(p, k, par)
                    s, h = e_head(p, k)
                    if live(s):
                        score_t(s, h, 1 - par if k >= LAG else par)
                    if k in (0, 3, 8) and live(p):
                        spread(p, 1 + (k + 1) // 4)
                    if k == 13 and live(p + 1):
                        spread(p + 1, 0)
                    if k == 12 and live(p - 1):
                        weigh(p - 1, 0, 1 - par)
                    if k in (0, 4, 8) and live(p - 2):
                        weigh(p - 2, 1 + k // 4, par)
                    if k == 2 and live(p - 1):
                        transpose_max(p - 1)
                    if k in (4, 7) and live(p - 1):
                        place_max(p - 1, k // 7, 1 - par)
                    if k in (11, 12) and live(p - 2):
                        project_out(p - 2, k - 11)
                    if live(p + 1):
                        if k == 1:
                            transpose_x(p + 1)
                        if k == 5:
                            project_qk(p + 1, 1 - par)
                        if k == 6:
                            project_swapped(p + 1, 1 - par)
                    if k == 14 and live(p):
                        project_v(p, par)

            periods(pe, period)

        @block.vector
        def _(dve):
            dve.wait_ge(const_in, 16 * N_CONST)
            nc.vector.tensor_copy(sel[:].rearrange("p a b c n -> p (a b c n)"), sel_raw[:]).then_inc(sel_set, 1)

            def norm_stats(s, st, mv, st_sem, mv_sem, done):
                if live(s - 1):
                    dve.wait_ge(mv_sem, count(s - 1, 2, 1))
                dve.sem_inc(dve_held, 1)
                for i in range(TILES):
                    nc.vector.bn_stats(st[:, i, :], tile(xa, s, i)).then_inc(st_sem, 1)
                if live(s - 1):
                    dve.wait_ge(done, count(s - 1, 1))
                for i in range(TILES):
                    dve.wait_ge(st_sem, count(s, 2, i))
                    dve.sem_inc(dve_held, 1)
                    nc.vector.bn_aggr(mv[:, i, :], st[:, i, :]).then_inc(mv_sem, 1)

            def row_max(s, h, par):
                dve.wait_ge(s_mm, count(s, 16, h))
                dve.sem_inc(dve_held, 1)
                for i, cols in enumerate((slice(0, 128), slice(128, 384))):
                    masked_max(nc, neg_max[par][:, i, h:h + 1], bank_s[h % 2][:, cols], mask_q[:, cols]).then_inc(max_set, 1)

            def cut_max(s, par):
                nm = neg_max[par]
                dve.wait_ge(max_set, 2 * count(s, 16, 15))
                if live(s - 1):
                    dve.wait_ge(mT_mm, count(s - 1, 1))
                nc.vector.tensor_copy(parts[:, :, 0:HA], nm[:]).then_inc(m_step, 1)
                dve.wait_ge(m_step, count(s, 5, 0))
                nc.vector.tensor_tensor(rest1[:], nm[:], parts[:, :, 0:HA], ALU.subtract).then_inc(m_step, 1)
                dve.wait_ge(m_step, count(s, 5, 1))
                nc.vector.tensor_copy(parts[:, :, HA:2 * HA], rest1[:]).then_inc(m_step, 1)
                dve.wait_ge(m_step, count(s, 5, 2))
                nc.vector.tensor_tensor(rest2[:], rest1[:], parts[:, :, HA:2 * HA], ALU.subtract).then_inc(m_step, 1)
                dve.wait_ge(m_step, count(s, 5, 3))
                nc.vector.tensor_copy(parts[:, :, 2 * HA:3 * HA], rest2[:]).then_inc(m_step, 1)

            def set_max(s, par):
                dve.wait_ge(mT_mm, count(s, 1))
                if live(s - 2):
                    dve.wait_ge(mx_mm, count(s - 2, 2, 1))
                nc.vector.tensor_copy(neg_maxT[par][:], partsT[0:3 * HA, :]).then_inc(mT_set, 1)

            def add_max(s, pair, par):
                dve.wait_ge(mx_mm, count(s, 2, pair))
                q = slots[par][:, 2 * pair:2 * pair + 2, 0, :]
                nc.vector.tensor_tensor(q, q.bitcast(F32), bank_m[:].rearrange("p (a t) -> p a t", a=2), ALU.add).then_inc(mx_set, 1)

            def normalize(s, c):
                dve.wait_ge(invd_set, count(s, 4, c))
                if c == 0 and live(s - 1):
                    dve.wait_ge(out_mm, count(s - 1, 2, 1))
                nc.vector.tensor_tensor(oT[:, c, :], bank_o[:, 0:T], inv_den[:], ALU.mult).then_inc(oT_set, 1)

            def period(p, par):
                for k in range(16):
                    if k == 3 and live(p - 1):
                        set_max(p - 1, 1 - par)
                    if k in (5, 8) and live(p - 1):
                        add_max(p - 1, k // 8, 1 - par)
                    if live(p):
                        row_max(p, k, par)
                    if k == 0 and live(p - 1):
                        cut_max(p - 1, 1 - par)
                    if k == 6 and live(p + 1):
                        dve.wait_ge(qk_mm, count(p + 1, 1))
                        if live(p):
                            dve.wait_ge(qk_set, count(p, 1))
                        nc.vector.tensor_tensor(rot_c[:], bank_6[:].rearrange("p (a t) -> p a t", a=2), rope_c[:],
                                                ALU.mult).then_inc(rot_c_set, 1)
                    if k == 7 and live(p + 1):
                        dve.wait_ge(swap_mm, count(p + 1, 1))
                        nc.vector.tensor_tensor(rot_s[:], bank_7[:].rearrange("p (a t) -> p a t", a=2), rope_s[:],
                                                ALU.mult).then_inc(rot_s_set, 1)
                    if k == 13 and live(p - 1):
                        normalize(p - 1, 0)
                    if k in (1, 5, 9) and live(p - 2):
                        normalize(p - 2, 1 + k // 4)
                    if k == 13 and live(p - 2):
                        dve.wait_ge(out_mm, count(p - 2, 2, 1))
                        nc.vector.tensor_tensor(xa[:, rows(p - 2), :], xa[:, rows(p - 2), :],
                                                bank_m[:, 0:T].rearrange("p (t d) -> p t d", d=D), ALU.add).then_inc(xa_set, 1)
                    if k == 14 and live(p - 2):
                        dve.wait_ge(xa_set, count(p - 2, 1))
                        norm_stats(p - 2, stats2, mean_var2, stats2_set, mv2_set, z_set)
                    if k == 4 and live(p + 2):
                        dve.wait_ge(x_in[par], landed(p + 2, par))
                        norm_stats(p + 2, stats, mean_var, stats_set, mv_set, xn_set)

            periods(dve, period)

        @block.scalar
        def _(act):
            nc.scalar.preload_act_table_set("natural_log_exp_and_others")
            act.wait_ge(const_set, 4)

            def rsqrt_var(s, mv, lv, rs, mv_sem, lv_sem, rs_sem, used):
                act.wait_ge(mv_sem, count(s, 2, 1))
                if live(s - 1):
                    act.wait_ge(rs_sem, count(s - 1, 1))
                nc.scalar.activation(lv[:], mv[:, :, 1], ACT.Ln, bias=eps[:, 0:1]).then_inc(lv_sem, 1)
                act.wait_ge(lv_sem, count(s, 1))
                if live(s - 1):
                    act.wait_ge(used, count(s - 1, 1))
                nc.scalar.activation(rs[:], lv[:], ACT.Exp, scale=-0.5).then_inc(rs_sem, 1)

            def exp_head(s, h):
                act.wait_ge(p_mm, count(s, 16, h))
                if h % 4 == 0 and (h >= 8 or live(s - 1)):
                    act.wait_ge(o_mm, count(s, 4, h // 4 - 2))
                nc.scalar.activation(probs[:, h % 8, :], bank_p[h % 2][:, 0:384], ACT.Exp, scale=SCALE_A).then_inc(p_exp, 1)

            def invert_den(s, c):
                act.wait_ge(o_mm, count(s, 4, c))
                if c > 0 or live(s - 1):
                    act.wait_ge(invd_set, count(s, 4, c - 1))
                nc.scalar.activation(log_den[:], bank_o[:, T:2 * T], ACT.Ln).then_inc(logd_set, 1)
                act.wait_ge(logd_set, count(s, 4, c))
                if c > 0 or live(s - 1):
                    act.wait_ge(oT_set, count(s, 4, c - 1))
                nc.scalar.activation(inv_den[:], log_den[:], ACT.Exp, scale=-1.0).then_inc(invd_set, 1)

            def set_slots(s, c, par):
                act.wait_ge(sel_mm, count(s, 4, c))
                if live(s - 2):
                    act.wait_ge(p_mm, count(s - 2, 16, 4 * c + 3))
                nc.scalar.activation(slots[par][:, c, 0, :], bank_6[:, 0:T], ACT.Copy).then_inc(slots_set, 1)
                nc.scalar.activation(slots[par][:, c, 1, :], bank_6[:, T:2 * T], ACT.Identity, bias=k_ones[:, 0:1]
                                     ).then_inc(slots_set, 1)

            def period(p, par):
                for k in range(16):
                    s, h = e_head(p, k)
                    if live(s):
                        exp_head(s, h)
                    if k in (0, 3, 8) and live(p):
                        set_slots(p, 1 + (k + 1) // 4, par)
                    if k == 13 and live(p + 1):
                        set_slots(p + 1, 0, 1 - par)
                    if k == 14 and live(p):
                        act.wait_ge(v_mm, count(p, 1))
                        if live(p - 2):
                            act.wait_ge(o_mm, count(p - 2, 4, 3))
                        nc.scalar.activation(v[par][:, :, :, 0:DA],
                                             bank_7[:, 0:T].rearrange("p (t h d) -> p t h d", t=2, d=DA),
                                             ACT.Copy).then_inc(v_set, 1)
                    if k == 12 and live(p - 1):
                        invert_den(p - 1, 0)
                    if k in (0, 4, 8) and live(p - 2):
                        invert_den(p - 2, 1 + k // 4)
                    if k == 1 and live(p + 1):
                        act.wait_ge(xT_mm, count(p + 1, 1))
                        if live(p - 1):
                            act.wait_ge(v_mm, count(p - 1, 1))
                        nc.scalar.activation(xT[1 - par][:], bank_7[:, 0:T], ACT.Copy).then_inc(xT_set, 1)
                    if k == 10 and live(p + 1):
                        act.wait_ge(qk_set, count(p + 1, 1))
                        if live(p):
                            act.wait_ge(sel_mm, count(p, 4, 3))
                        nc.scalar.activation(qk_hi[:], qk[:], ACT.Copy).then_inc(hi_set, 1)
                    if k == 15 and live(p - 2):
                        rsqrt_var(p - 2, mean_var2, log_var2, rstd2, mv2_set, logv2_set, rstd2_set, z_set)
                    if k == 5 and live(p + 2):
                        rsqrt_var(p + 2, mean_var, log_var, rstd, mv_set, logv_set, rstd_set, xn_set)

            periods(act, period)


def window_stage(nc, t, m, banks, w, layer):
    z, ident, identb = m["z"], m["ident"], m["identb"]
    bank_s, bank_p, bank_o, bank_m, bank_6, bank_7 = banks[0:2], banks[2:4], banks[4], banks[5], banks[6], banks[7]
    partsT = bank_m[:, 0:T // 2].bitcast(BF16)
    g = w
    s_ = w["sems"]

    def count(seq, per_seq, unit=0):
        return (layer * SEQS + seq) * per_seq + unit + 1

    def periods(eng, period):
        for p in range(-2, 4):
            period(p, p % 2)
        with eng.Fori(2, (SEQS - 2) // 2) as i:
            for par in range(2):
                period(i * 2 + par, par)
        for p in range(SEQS - 2, SEQS + 2):
            period(p, p % 2)

    def rows(seq):
        return bass.ds(seq * TILES, TILES) if not isinstance(seq, int) else slice(seq * TILES, seq * TILES + TILES)

    def e_head(p, k):
        return (p - 1, k - 2) if k >= 2 else (p - 2, 6 + k)

    UNITS = ("q heads 0-3", "k heads 0-3", "q heads 4-7", "k heads 4-7")

    with nc.Block() as block:
        @block.sync
        def _(sp):
            for name in ("w_qk", "w_v", "w_o", "scales"):
                sp.dma_start(g[name] if name in ("w_qk", "w_v") else g[name][:], t["b_" + name][bass.ds(layer, 1)].rearrange("l p n -> p (l n)")).then_inc(s_["w_in"], 16)

        @block.gpsimd
        def _(pool):
            def period(p, par):
                for k in range(8):
                    if k == 4 and live(p + 2):
                        pool.wait_ge(s_["hT_hi"], count(p + 2, 1))
                        if live(p):
                            pool.wait_ge(s_["v_mm"], count(p, 2, 1))
                        nc.gpsimd.tensor_tensor(g["hT_lo"][par][:], g["hT"][:], g["hT_hi"][par][:].bitcast(F32),
                                                ALU.subtract).then_inc(s_["hT_lo"], 1)
                    s, u = (p + 1, k // 2 + 1) if k < 6 else (p + 2, 0)
                    if k % 2 == 0 and live(s):
                        pool.wait_ge(s_["rot"], count(s, 8, 2 * u + 1))
                        if live(s - 1):
                            pool.wait_ge(s_["normed"], count(s - 1, 4, u))
                        for half in range(2):
                            nc.gpsimd.tensor_tensor(g["unit"][u][:, half, :], g["rot_c"][u % 2][:, half, :],
                                                    g["rot_s"][u % 2][:, 1 - half, :], ALU.add).then_inc(s_["summed"], 1)
                    if k == 1 and live(p + 2):
                        if live(p + 1):
                            pool.wait_ge(s_["hT_mm"], count(p + 1, 1))
                        pool.sem_inc(s_["pool_held"], 1)
                        nc.gpsimd.tensor_copy(g["z_in"][:], z[:, rows(p + 2), :]).then_inc(s_["z_in"], 1)
                    if k == 5 and live(p + 1):
                        pool.wait_ge(s_["rn_hi"], count(p + 1, 1))
                        if live(p):
                            pool.wait_ge(s_["rep_mm"], count(p, 2, 1))
                        nc.gpsimd.tensor_tensor(g["rn_lo"][:], g["rn"][:], g["rn_hi"][:].bitcast(F32),
                                                ALU.subtract).then_inc(s_["rn_lo"], 1)

            periods(pool, period)

        @block.tensor
        def _(pe):
            pe.wait_ge(s_["w_in"], 64 * (layer + 1))
            pe.wait_ge(s_["w_lo"], 2 * (layer + 1))

            def transpose_z(s):
                pe.wait_ge(s_["z_in"], count(s, 1))
                if live(s - 3):
                    pe.wait_ge(s_["mT"], count(s - 3, 1))
                elif live(s - 2):
                    pe.wait_ge(s_["ssq"], count(s - 2, 1))
                elif live(s - 1):
                    pe.wait_ge(s_["hT_psum"], count(s - 1, 2, 1))
                for i in range(TILES):
                    last = nc.tensor.transpose(bank_m[:, i * 128:(i + 1) * 128], g["z_in"][:, i, :], ident[:])
                last.then_inc(s_["hT_mm"], 1)

            def project_qk(s, u, par):
                if u == 0:
                    pe.wait_ge(s_["hT_lo"], count(s, 1))
                if u > 0 or live(s - 1):
                    pe.wait_ge(s_["rot"], count(s, 8, 2 * u - 1))
                for half in range(2):
                    dst, c = bank_6[:, half * T:(half + 1) * T], slice((2 * u + half) * 128, (2 * u + half + 1) * 128)
                    nc.tensor.matmul(dst, g["w_qk_hi"][:, c], g["hT_hi"][par][:], start=True, stop=False)
                    nc.tensor.matmul(dst, g["w_qk_hi"][:, c], g["hT_lo"][par][:], start=False, stop=False)
                    last = nc.tensor.matmul(dst, g["w_qk_lo"][:, c], g["hT_hi"][par][:], start=False, stop=True)
                last.then_inc(s_["qk_mm"], 1)

            def project_v(s, i, par):
                if i == 0:
                    pe.wait_ge(s_["normed"], count(s, 4, 3))
                if i == 1:
                    pe.wait_ge(s_["v"], count(s, 2, 0))
                hi, lo = (g[part][par][:, i * 128:(i + 1) * 128] for part in ("hT_hi", "hT_lo"))
                nc.tensor.matmul(bank_7[:], hi, g["w_v_hi"][:], start=True, stop=False)
                nc.tensor.matmul(bank_7[:], hi, g["w_v_lo"][:], start=False, stop=False)
                nc.tensor.matmul(bank_7[:], lo, g["w_v_hi"][:], start=False, stop=True).then_inc(s_["v_mm"], 1)

            def sum_squares(s):
                pe.wait_ge(s_["squares"], count(s, 4, 3))
                if live(s + 1):
                    pe.wait_ge(s_["hT_psum"], count(s + 1, 2, 1))
                else:
                    pe.wait_ge(s_["mT"], count(s - 2, 1))
                for half in range(2):
                    for u in range(4):
                        last = nc.tensor.matmul(bank_m[32 * u:32 * u + 32, 0:T], g["head_sum"][:], g["sq"][u][:, half, :],
                                                start=(half == 0), stop=(half == 1), skip_group_check=True)
                last.then_inc(s_["ssq_mm"], 1)

            def repeat_norms(s, pair):
                pe.wait_ge(s_["rn_lo"], count(s, 1))
                if pair == 1:
                    pe.wait_ge(s_["normed"], count(s, 4, 1))
                elif live(s - 1):
                    pe.wait_ge(s_["v"], count(s - 1, 2, 1))
                for i in range(2):
                    dst, rep = bank_7[:, i * T:(i + 1) * T], g["head_rep_r"][:, (2 * pair + i) * 128:(2 * pair + i + 1) * 128]
                    nc.tensor.matmul(dst, rep, g["rn_hi"][:], start=True, stop=False)
                    last = nc.tensor.matmul(dst, rep, g["rn_lo"][:], start=False, stop=True)
                last.then_inc(s_["rep_mm"], 1)

            def score(s, h, par):
                if h % 4 == 0:
                    pe.wait_ge(s_["moved_q"], count(s, 8, h + 3))
                    pe.wait_ge(s_["moved_k"], count(s, 8, h + 3))
                if h >= 2 or live(s - 1):
                    pe.wait_ge(s_["den"], 2 * count(s, 8, h - 2))
                r = slice(64 * (h % 2), 64 * (h % 2) + 64)
                q, k, bank = g["heads"][par][r, 0, h // 2, :], g["heads"][par][r, 1, h // 2, :], bank_s[h % 2]
                nc.tensor.matmul(bank[:, 0:128], q[:, 0:128], k[:, 0:128], start=True, stop=False, skip_group_check=True)
                nc.tensor.matmul(bank[:, 128:320], q[:, 128:256], k[:, 64:256], start=False, stop=True,
                                 skip_group_check=True).then_inc(s_["s_mm"], 1)

            def score_t(s, h, par):
                if h == 0:
                    pe.wait_ge(s_["mT"], count(s, 1))
                if h >= 2 or live(s - 1):
                    pe.wait_ge(s_["p"], count(s, 8, h - 2))
                r = slice(64 * (h % 2), 64 * (h % 2) + 64)
                q, k, bank = g["heads"][par][r, 0, h // 2, :], g["heads"][par][r, 1, h // 2, :], bank_p[h % 2]
                nm = g["neg_maxT"][par]
                nc.tensor.matmul(bank[:, 0:192], k[:, 0:128], q[:, 0:192], start=True, stop=False, skip_group_check=True)
                nc.tensor.matmul(bank[:, 192:320], k[:, 128:256], q[:, 128:256], start=False, stop=False, skip_group_check=True)
                nc.tensor.matmul(bank[:, 0:192], g["head_row"][:, h, :], nm[:, 0:192], start=False, stop=False, skip_group_check=True)
                nc.tensor.matmul(bank[:, 192:320], g["head_row"][:, h, :], nm[:, 128:256], start=False, stop=False, skip_group_check=True)
                nc.tensor.matmul(bank[:, 0:320], identb[:], g["mask_k"][:], start=False, stop=True,
                                 skip_group_check=True).then_inc(s_["p_mm"], 1)

            def weigh(s, c, par):
                pe.wait_ge(s_["p"], count(s, 8, 2 * c + 1))
                if c == 0:
                    pe.wait_ge(s_["v"], count(s, 2, 1))
                if c > 0 or live(s - 1):
                    pe.wait_ge(s_["oT"], count(s, 4, c - 1))
                for kt in range(2):
                    for a in range(2):
                        h = 2 * c + a
                        src = g["probs"][:, h % 4, 192:320] if kt else g["probs"][:, h % 4, 0:192]
                        last = nc.tensor.matmul(bank_o[64 * a:64 * a + 64, (128 if kt else 0):(256 if kt else 192)],
                                                g["v"][par][:, kt, h * DB:(h + 1) * DB], src, start=(kt == 0), stop=(kt == 1),
                                                skip_group_check=True)
                last.then_inc(s_["o_mm"], 1)

            def transpose_max(s):
                pe.wait_ge(s_["cut"], count(s, 6, 5))
                if live(s - 2):
                    pe.wait_ge(s_["z_set"], count(s - 2, 1))
                elif live(s + 1):
                    pe.wait_ge(s_["ssq"], count(s + 1, 1))
                pe.sem_inc(s_["pe_held"], 1)
                for i in range(2):
                    last = nc.tensor.transpose(partsT[0:3 * HB, i * 128:(i + 1) * 128], g["parts"][:, i, :], identb[:])
                last.then_inc(s_["mT_mm"], 1)

            def project_out(s, i, par):
                pe.wait_ge(s_["oT"], count(s, 4, 3))
                if i == 1:
                    pass
                elif live(s + 3):
                    pe.wait_ge(s_["ssq"], count(s + 3, 1))
                elif live(s + 1):
                    pe.wait_ge(s_["mT"], count(s + 1, 1))
                elif live(s - 1):
                    pe.wait_ge(s_["z_set"], count(s - 1, 1))
                for c in range(4):
                    last = nc.tensor.matmul(bank_m[:, i * 128:(i + 1) * 128], g["oT"][par][:, c, i * 128:(i + 1) * 128],
                                            g["w_o"][:, c * D:(c + 1) * D], start=(c == 0), stop=(c == 3))
                last.then_inc(s_["out_mm"], 1)

            def period(p, par):
                for k in range(8):
                    if live(p):
                        score(p, k, par)
                    if k == 6 and live(p + 1):
                        repeat_norms(p + 1, 0)
                    s, h = e_head(p, k)
                    if live(s):
                        score_t(s, h, 1 - par if k >= 2 else par)
                    if k == 4 and live(p + 1):
                        sum_squares(p + 1)
                    if k in (0, 2) and live(p - 2):
                        weigh(p - 2, 2 + k // 2, par)
                    if k in (4, 6) and live(p - 1):
                        weigh(p - 1, k // 2 - 2, 1 - par)
                    if k in (1, 3) and live(p + 1):
                        project_qk(p + 1, 2 + k // 2, 1 - par)
                    if k in (2, 3) and live(p):
                        project_v(p, k - 2, par)
                    if k == 0 and live(p):
                        repeat_norms(p, 1)
                    if k == 0 and live(p - 1):
                        transpose_max(p - 1)
                    if k == 2 and live(p + 2):
                        transpose_z(p + 2)
                    if k in (5, 7) and live(p + 2):
                        project_qk(p + 2, k // 2 - 2, par)
                    if k in (6, 7) and live(p - 2):
                        project_out(p - 2, k - 6, par)

            periods(pe, period)

        @block.vector
        def _(dve):
            dve.wait_ge(s_["w_in"], 64 * (layer + 1))
            for side in range(2):
                for half in range(2):
                    sc = g["scales"][:, 2 * side + half:2 * side + half + 1]
                    nc.vector.tensor_scalar(g["tab_c"][:, side, half, :], g["rope"][:, side, 0, :], sc, None,
                                            ALU.mult).then_inc(s_["tables"], 1)
                    nc.vector.tensor_scalar(g["tab_s"][:, side, half, :], g["rope"][:, side, 1, :], sc, -1.0 if half else 1.0,
                                            ALU.mult, ALU.mult).then_inc(s_["tables"], 1)
            dve.wait_ge(s_["w_hi"], 2 * (layer + 1))
            for name in ("w_qk", "w_v"):
                nc.vector.tensor_tensor(g[name + "_lo"][:], g[name], g[name + "_hi"][:].bitcast(F32),
                                        ALU.subtract).then_inc(s_["w_lo"], 1)
            dve.wait_ge(s_["tables"], 8 * (layer + 1))

            def row_max(s, h, par):
                dve.wait_ge(s_["s_mm"], count(s, 8, h))
                dve.sem_inc(s_["dve_held"], 1)
                for i, cols in enumerate((slice(0, 128), slice(128, 320))):
                    masked_max(nc, g["neg_max"][par][:, i, h:h + 1], bank_s[h % 2][:, cols], g["mask_q"][:, cols]
                               ).then_inc(s_["max"], 1)

            def cut_max(s, par):
                shift, parts, rest = g["shift"], g["parts"], g["rest"]
                dve.wait_ge(s_["log_sum"], count(s, 1))
                dve.wait_ge(s_["max"], 2 * count(s, 8, 7))
                if live(s - 1):
                    dve.wait_ge(s_["cut"], count(s - 1, 6, 5))
                nc.vector.tensor_tensor(shift[:], g["neg_max"][par][:], g["log_sum"][:], ALU.subtract).then_inc(s_["cut"], 1)
                dve.wait_ge(s_["cut"], count(s, 6, 0))
                if live(s - 1):
                    dve.wait_ge(s_["mT_mm"], count(s - 1, 1))
                nc.vector.tensor_copy(parts[:, :, 0:HB], shift[:]).then_inc(s_["cut"], 1)
                dve.wait_ge(s_["cut"], count(s, 6, 1))
                nc.vector.tensor_tensor(rest[0][:], shift[:], parts[:, :, 0:HB], ALU.subtract).then_inc(s_["cut"], 1)
                dve.wait_ge(s_["cut"], count(s, 6, 2))
                nc.vector.tensor_copy(parts[:, :, HB:2 * HB], rest[0][:]).then_inc(s_["cut"], 1)
                dve.wait_ge(s_["cut"], count(s, 6, 3))
                nc.vector.tensor_tensor(rest[1][:], rest[0][:], parts[:, :, HB:2 * HB], ALU.subtract).then_inc(s_["cut"], 1)
                dve.wait_ge(s_["cut"], count(s, 6, 4))
                nc.vector.tensor_copy(parts[:, :, 2 * HB:3 * HB], rest[1][:]).then_inc(s_["cut"], 1)

            def set_max(s, par):
                dve.wait_ge(s_["mT_mm"], count(s, 1))
                if live(s - 2):
                    dve.wait_ge(s_["p_mm"], count(s - 2, 8, 7))
                nc.vector.tensor_copy(g["neg_maxT"][par][:], partsT[0:3 * HB, :]).then_inc(s_["mT"], 1)

            def rotate(s, u):
                dve.wait_ge(s_["squares"], count(s, 4, u))
                if u >= 2 or live(s - 1):
                    dve.wait_ge(s_["summed"], 2 * count(s, 4, u - 2))
                src = bank_6[:].rearrange("p (a t) -> p a t", a=2)
                nc.vector.tensor_tensor(g["rot_c"][u % 2][:], src, g["tab_c"][:, u % 2], ALU.mult).then_inc(s_["rot"], 1)
                nc.vector.tensor_tensor(g["rot_s"][u % 2][:], src, g["tab_s"][:, u % 2], ALU.mult).then_inc(s_["rot"], 1)

            def clip_squares(s):
                dve.wait_ge(s_["ssq_mm"], count(s, 1))
                if live(s - 1):
                    dve.wait_ge(s_["log_norm"], count(s - 1, 1))
                nc.vector.tensor_scalar(g["ssq"][:], bank_m[:, 0:T], NORM_MIN ** 2, None, ALU.max).then_inc(s_["ssq"], 1)

            def apply_norms(s, pair, par):
                dve.wait_ge(s_["rep_mm"], count(s, 2, pair))
                dve.wait_ge(s_["summed"], 2 * count(s, 4, 2 * pair + 1))
                if live(s - 2):
                    dve.wait_ge(s_["p_mm"], count(s - 2, 8, 4 * pair + 3))
                if pair == 1 or live(s - 1):
                    dve.wait_ge(s_["moved_q"], count(s, 8, 4 * pair - 1))
                    dve.wait_ge(s_["moved_k"], count(s, 8, 4 * pair - 1))
                for side in range(2):
                    u = g["unit"][2 * pair + side]
                    rn = bank_7[:, side * T:(side + 1) * T]
                    nc.vector.tensor_tensor(g["heads"][par][:, side, 2 * pair:2 * pair + 2, :],
                                            u[:, 0, :].unsqueeze(1).broadcast_to([128, 2, T]),
                                            rn.unsqueeze(1).broadcast_to([128, 2, T]), ALU.mult).then_inc(s_["in_place"], 1)
                    nc.vector.tensor_tensor(g["half_2"][side][:], u[:, 1, :], rn, ALU.mult).then_inc(s_["normed"], 1)

            def move_k(s, pair, par):
                dve.wait_ge(s_["normed"], count(s, 4, 2 * pair + 1))
                dve.wait_ge(s_["in_place"], count(s, 4, 2 * pair + 1))
                for b in range(4):
                    to = 32 * (b ^ 1)
                    nc.vector.tensor_copy(g["heads"][par][to:to + 32, 1, 2 * pair + b % 2, :],
                                          g["half_2"][1][32 * b:32 * b + 32, :]).then_inc(s_["moved_k"], 1)

            def set_oT(s, c, par):
                dve.wait_ge(s_["o_mm"], count(s, 4, c))
                if c == 0 and live(s - 2):
                    dve.wait_ge(s_["out_mm"], count(s - 2, 2, 1))
                nc.vector.tensor_copy(g["oT"][par][:, c, :], bank_o[:, 0:T]).then_inc(s_["oT"], 1)

            def add_out(s):
                dve.wait_ge(s_["out_mm"], count(s, 2, 1))
                nc.vector.tensor_tensor(z[:, rows(s), :], z[:, rows(s), :],
                                        bank_m[:, 0:T].rearrange("p (t d) -> p t d", d=D), ALU.add).then_inc(s_["z_set"], 1)

            def half_stats(s):
                dve.wait_ge(s_["z_set"], count(s, 1))
                dve.sem_inc(s_["dve_held"], 1)
                for i in range(TILES):
                    for half in range(2):
                        nc.vector.bn_stats(m["half_stats"][:, half, s * TILES + i, :],
                                           z[:, s * TILES + i, half * 64:half * 64 + 64]).then_inc(s_["half_stats"], 1)

            def period(p, par):
                for k in range(8):
                    if k == 7 and live(p + 1):
                        move_k(p + 1, 0, 1 - par)
                    if k == 0 and live(p - 1):
                        cut_max(p - 1, 1 - par)
                    if k == 1 and live(p - 1):
                        set_max(p - 1, 1 - par)
                    if k in (1, 3) and live(p - 2):
                        set_oT(p - 2, 2 + k // 2, par)
                    if k in (5, 7) and live(p - 1):
                        set_oT(p - 1, k // 2 - 2, 1 - par)
                    if k == 1 and live(p):
                        apply_norms(p, 1, par)
                    if live(p):
                        row_max(p, k, par)
                    if k in (0, 2, 4) and live(p + 1):
                        rotate(p + 1, k // 2 + 1)
                    if k == 2 and live(p):
                        move_k(p, 1, par)
                    if k == 4 and live(p + 1):
                        clip_squares(p + 1)
                    if k == 6 and live(p + 2):
                        rotate(p + 2, 0)
                    if k == 6 and live(p + 1):
                        apply_norms(p + 1, 0, 1 - par)
                    if k == 7 and live(p - 2):
                        add_out(p - 2)
                    if k == 3 and live(p - 3):
                        half_stats(p - 3)

            periods(dve, period)
            half_stats(SEQS - 1)

        @block.scalar
        def _(act):
            nc.scalar.preload_act_table_set("natural_log_exp_and_others")
            act.wait_ge(s_["w_in"], 64 * (layer + 1))
            for name in ("w_qk", "w_v"):
                nc.scalar.activation(g[name + "_hi"][:], g[name], ACT.Copy).then_inc(s_["w_hi"], 1)

            def exp_head(s, h):
                act.wait_ge(s_["p_mm"], count(s, 8, h))
                if h % 2 == 0 and (h >= 4 or live(s - 1)):
                    act.wait_ge(s_["o_mm"], count(s, 4, h // 2 - 2))
                nc.scalar.activation(g["probs"][:, h % 4, :], bank_p[h % 2][:, 0:320], ACT.Exp).then_inc(s_["p"], 1)

            def square(s, u):
                act.wait_ge(s_["qk_mm"], count(s, 4, u))
                if live(s - 1):
                    act.wait_ge(s_["ssq_mm"], count(s - 1, 1))
                elif u == 0:
                    act.wait_ge(s_["w_lo"], 2 * (layer + 1))
                nc.scalar.activation(g["sq"][u], bank_6[:].rearrange("p (a t) -> p a t", a=2), ACT.Square).then_inc(s_["squares"], 1)

            def move_q(s, pair, par):
                act.wait_ge(s_["normed"], count(s, 4, 2 * pair))
                act.wait_ge(s_["in_place"], count(s, 4, 2 * pair))
                for b in range(4):
                    to = 32 * (b ^ 1)
                    nc.scalar.activation(g["heads"][par][to:to + 32, 0, 2 * pair + b % 2, :],
                                         g["half_2"][0][32 * b:32 * b + 32, :], ACT.Copy).then_inc(s_["moved_q"], 1)

            def invert_norms(s):
                act.wait_ge(s_["ssq"], count(s, 1))
                if live(s - 1):
                    act.wait_ge(s_["rnorm"], count(s - 1, 1))
                nc.scalar.activation(g["log_ssq"][:], g["ssq"][:], ACT.Ln, scale=NORM_SHIFT ** 2).then_inc(s_["log_norm"], 1)
                act.wait_ge(s_["log_norm"], count(s, 1))
                if live(s - 1):
                    act.wait_ge(s_["rn_lo"], count(s - 1, 1))
                nc.scalar.activation(g["rn"][:], g["log_ssq"][:], ACT.Exp, scale=-0.5).then_inc(s_["rnorm"], 1)
                act.wait_ge(s_["rnorm"], count(s, 1))
                if live(s - 1):
                    act.wait_ge(s_["rep_mm"], count(s - 1, 2, 1))
                nc.scalar.activation(g["rn_hi"][:], g["rn"][:], ACT.Copy).then_inc(s_["rn_hi"], 1)

            def row_sum(s, h, par):
                act.wait_ge(s_["max"], 2 * count(s, 8, h))
                for i, cols in enumerate((slice(0, 128), slice(128, 320))):
                    neg_scores = bank_s[h % 2][:, cols]
                    nc.scalar.activation(neg_scores, neg_scores, ACT.Exp, scale=-1.0, bias=g["neg_max"][par][:, i, h:h + 1],
                                         accum_out=g["den"][par][:, i, h:h + 1]).then_inc(s_["den"], 1)

            def log_sums(s, par):
                act.wait_ge(s_["den"], 2 * count(s, 8, 7))
                if live(s - 1):
                    act.wait_ge(s_["cut"], count(s - 1, 6, 0))
                nc.scalar.activation(g["log_sum"][:], g["den"][par][:], ACT.Ln).then_inc(s_["log_sum"], 1)

            def set_hT(s):
                act.wait_ge(s_["hT_mm"], count(s, 1))
                if live(s - 1):
                    act.wait_ge(s_["hT_lo"], count(s - 1, 1))
                nc.scalar.activation(g["hT"][0:64, :], bank_m[0:64, 0:T], ACT.Copy).then_inc(s_["hT_psum"], 1)
                nc.scalar.activation(g["hT"][64:128, 1:T], bank_m[64:128, 0:T - 1], ACT.Copy).then_inc(s_["hT_psum"], 1)

            def high_hT(s, par):
                act.wait_ge(s_["hT_psum"], count(s, 2, 1))
                if live(s - 2):
                    act.wait_ge(s_["v_mm"], count(s - 2, 2, 1))
                nc.scalar.activation(g["hT_hi"][par][:], g["hT"][:], ACT.Copy).then_inc(s_["hT_hi"], 1)

            def set_v(s, i, par):
                act.wait_ge(s_["v_mm"], count(s, 2, i))
                if live(s - 2):
                    act.wait_ge(s_["o_mm"], count(s - 2, 4, 3))
                nc.scalar.activation(g["v"][par][:, i, :], bank_7[:], ACT.Copy).then_inc(s_["v"], 1)

            def period(p, par):
                for k in range(8):
                    s, h = e_head(p, k)
                    if k == 3 and live(p + 2):
                        set_hT(p + 2)
                    if k == 4 and live(p + 2):
                        high_hT(p + 2, par)
                    if k == 7 and live(p + 1):
                        move_q(p + 1, 0, 1 - par)
                    if live(s):
                        exp_head(s, h)
                    if k == 1 and live(p):
                        move_q(p, 1, par)
                    if live(p):
                        row_sum(p, k, par)
                    if k == 7 and live(p):
                        log_sums(p, par)
                    if k == 4 and live(p + 1):
                        invert_norms(p + 1)
                    if k in (1, 3) and live(p + 1):
                        square(p + 1, 2 + k // 2)
                    if k in (2, 3) and live(p):
                        set_v(p, k - 2, par)
                    if k in (5, 7) and live(p + 2):
                        square(p + 2, k // 2 - 2)

            periods(act, period)


def window_buffers(nc, ctx):
    def sb(name, shape, dt=F32):
        return ctx.enter_context(nc.sbuf_tensor("b_" + name, shape, dt))

    g = {name: sb(name, shape) for name, shape in dict(
        sq_all=[128, 4 * 2 * T], w_o=[128, 4 * D], scales=[128, 4],
        rope=[128, 2, 2, T], tab_c=[128, 2, 2, T], tab_s=[128, 2, 2, T],
        head_sum=[128, 32],
        z_in=[128, TILES, D], ssq=[128, T], log_ssq=[128, T], rn=[128, T],
        probs=[128, 4, 320], log_sum=[128, 2, HB], shift=[128, 2, HB], hT=[128, T],
    ).items()}
    for name, shape, n in (("oT", [128, 4, T], 2), ("rot_c", [128, 2, T], 2), ("rot_s", [128, 2, T], 2), ("half_2", [128, T], 2), ("unit", [128, 2, T], 4),
                           ("heads", [128, 2, 4, T], 2), ("v", [128, TILES, HB * DB], 2),
                           ("neg_max", [128, 2, HB], 2), ("den", [128, 2, HB], 2), ("rest", [128, 2, HB], 2)):
        g[name] = [sb(f"{name}{i}", shape) for i in range(n)]
    sq = g["sq_all"]
    g["sq"] = [sq[:, u * 2 * T:(u + 1) * 2 * T].rearrange("p (a t) -> p a t", a=2) for u in range(4)]
    g["w_qk"], g["w_v"], g["head_rep"] = sq[:, 0:8 * 128], sq[:, 8 * 128:8 * 128 + HB * DB], sq[:, 0:4 * 128]
    for name, width in (("w_qk", 8 * 128), ("w_v", HB * DB), ("rn", T)):
        for part in ("_hi", "_lo"):
            g[name + part] = sb(name + part, [128, width], F32R)
    for part in ("hT_hi", "hT_lo"):
        g[part] = [sb(f"{part}{i}", [128, T], F32R) for i in range(2)]
    g["head_rep_r"] = sb("head_rep_r", [128, 4 * 128], F32R)
    g["mask_q"] = sb("mask_q", [128, 320])
    g["mask_k"] = sb("mask_k", [128, 320], BF16)
    g["head_row"] = sb("head_row", [3 * HB, HB, 128], BF16)
    g["parts"] = sb("parts", [128, 2, 3 * HB], BF16)
    g["neg_maxT"] = [sb(f"neg_maxT{i}", [3 * HB, T], BF16) for i in range(2)]
    names = """w_in in_place normed moved_q moved_k p_mm rot summed hT_mm z_in z_set ssq hT_psum hT_hi hT_lo rn_hi rn_lo w_hi w_lo v v_mm qk_mm squares ssq_mm mT rnorm rep_mm
        max s_mm p oT o_mm cut mT_mm out_mm tables log_norm den log_sum half_stats pe_held dve_held pool_held""".split()
    g["sems"] = {name: ctx.enter_context(nc.semaphore("b_" + name)) for name in names}
    return g


def mlp_stage(nc, t, m, banks, w, layer, out):
    z, xa, ident = m["z"], m["xa"], m["ident"]
    g = w
    s_ = w["sems"]
    N = SEQS * TILES
    stats, mv, rb, rb_next = m["half_stats"], g["mv"], g["rb"], g["rb_next"]

    def count(seq, per_seq, unit=0):
        return (layer * SEQS + seq) * per_seq + unit + 1

    def rows(seq):
        return bass.ds(seq * TILES, TILES) if not isinstance(seq, int) else slice(seq * TILES, seq * TILES + TILES)

    def by_tile(a):
        return a.rearrange("p (s i) -> p i s", i=TILES)

    with nc.Block() as block:
        @block.sync
        def _(sp):
            for name in ("w_1", "w_2", "b_1", "norm"):
                sp.dma_start(g[name][:], t["c_" + name][bass.ds(layer, 1)].rearrange("l p n -> p (l n)")).then_inc(s_["w_in"], 16)
            sp.dma_start(g["b_2"][:], t["L0_ffn_b2"][bass.ds(layer, 1)].broadcast_to([128, D])).then_inc(s_["w_in"], 16)
            sp.wait_ge(s_["zero_stats"], layer + 1)
            sp.dma_start(g["moved"][1:128, :, :], stats[0:127, 1, :, :]).then_inc(s_["stats_in"], 16)
            odd, even = slice(1, N, 2), slice(0, N, 2)
            sp.dma_start(g["moved"][0:1, odd, :], stats[127:128, 1, even, :]).then_inc(s_["stats_in"], 16)
            sp.wait_ge(s_["rb"], 2 * (layer + 1))
            sp.dma_start(rb_next[0:127], rb[1:128]).then_inc(s_["next_in"], 16)
            sp.dma_start(rb_next[127:128, :, 0, :], rb[0:1, :, 1, :]).then_inc(s_["next_in"], 16)
            sp.dma_start(rb_next[127:128, 1, 1, :], rb[0:1, 1, 0, :]).then_inc(s_["next_in"], 16)
            sp.dma_start(rb_next[127:128, 0, 1, :], g["zeros"][0:1, 0:SEQS]).then_inc(s_["next_in"], 16)
            sp.wait_ge(s_["next_in"], 64 * (layer + 1))
            sp.sem_inc(s_["sp_held"], 1)
            sp.wait_ge(s_["w_in"], 80 * (layer + 1))
            sp.sem_inc(s_["sp_held"], 1)

        @block.vector
        def _(dve):
            nc.vector.bn_stats(g["zero_stats"][:], g["zeros"][0:1, 0:64]).then_inc(s_["zero1"], 1)
            dve.wait_ge(s_["zero1"], layer + 1)
            nc.vector.tensor_copy(g["moved"][0:1, 0:N:2, :], g["zero_stats"][:].unsqueeze(1).broadcast_to([1, N // 2, 6])
                                  ).then_inc(s_["zero_stats"], 1)
            dve.wait_ge(s_["zero_stats"], layer + 1)
            dve.wait_ge(s_["stats_in"], 32 * (layer + 1))
            nc.vector.tensor_copy(stats[:, 1, :, :], g["moved"][:]).then_inc(s_["stats_set"], 1)
            dve.wait_ge(s_["stats_set"], layer + 1)
            means, squares = (stats[:, :, :, i:6:3].rearrange("p h n e -> p n h e") for i in (1, 2))
            steps = layer * 7
            nc.vector.tensor_reduce(g["sums"][:, 0], means, AX.XY, ALU.add).then_inc(s_["mv"], 1)
            nc.vector.tensor_reduce(g["sums"][:, 1], squares, AX.XY, ALU.add).then_inc(s_["mv"], 1)
            dve.wait_ge(s_["mv"], steps + 2)
            nc.vector.tensor_scalar(mv[:, :, 0], g["sums"][:, 0], 0.25, None, ALU.mult).then_inc(s_["mv"], 1)
            dve.wait_ge(s_["mv"], steps + 3)
            by_group = lambda a: a.rearrange("p n (h e) -> p n h e", h=2)
            nc.vector.tensor_tensor(by_group(g["dev"][:]), means, mv[:, :, 0:1].unsqueeze(3).broadcast_to([128, N, 2, 2]),
                                    ALU.subtract).then_inc(s_["mv"], 1)
            dve.wait_ge(s_["mv"], steps + 4)
            nc.vector.tensor_tensor(g["dev2"][:], g["dev"][:], g["dev"][:], ALU.mult).then_inc(s_["mv"], 1)
            dve.wait_ge(s_["mv"], steps + 5)
            nc.vector.tensor_reduce(g["sums"][:, 0], g["dev2"][:], AX.X, ALU.add).then_inc(s_["mv"], 1)
            dve.wait_ge(s_["mv"], steps + 6)
            nc.vector.scalar_tensor_tensor(out=mv[:, :, 1], in0=g["sums"][:, 0], scalar=float(D // 4), in1=g["sums"][:, 1],
                                           op0=ALU.mult, op1=ALU.add).then_inc(s_["mv"], 1)
            dve.wait_ge(s_["w_hi"], layer + 1)
            nc.vector.tensor_tensor(g["w_1_lo"], g["w_1"][:], g["w_1_hi"].bitcast(F32), ALU.subtract).then_inc(s_["w_lo"], 1)
            dve.wait_ge(s_["rb_r"], layer + 1)
            nc.vector.scalar_tensor_tensor(out=rb[:, 1], in0=by_tile(mv[:, :, 0]), scalar=-1.0, in1=rb[:, 0], op0=ALU.mult,
                                           op1=ALU.mult).then_inc(s_["rb"], 2)

        @block.scalar
        def _(act):
            nc.scalar.preload_act_table_set("natural_log_exp_and_others")
            act.wait_ge(s_["w_in"], 80 * (layer + 1))
            nc.scalar.activation(g["w_1_hi"], g["w_1"][:], ACT.Copy).then_inc(s_["w_hi"], 1)
            act.wait_ge(s_["mv"], 7 * (layer + 1))
            nc.scalar.activation(g["log_var"][:], by_tile(mv[:, :, 1]), ACT.Ln, scale=1.0 / D, bias=m["eps"][:, 0:1]).then_inc(s_["log_var"], 1)
            act.wait_ge(s_["log_var"], layer + 1)
            nc.scalar.activation(rb[:, 0], g["log_var"][:], ACT.Exp, scale=-0.5).then_inc(s_["rb_r"], 1)

    def periods(eng, period):
        for p in range(-2, 4):
            period(p, p % 2)
        with eng.Fori(2, (SEQS - 2) // 2) as i:
            for par in range(2):
                period(i * 2 + par, par)
        for p in range(SEQS - 2, SEQS + 2):
            period(p, p % 2)

    bank_g, bank_a, bank_2 = banks[0:2], banks[2:4], banks[4:6]
    bank_t, bank_o = banks[6], banks[7]

    with nc.Block() as block:
        @block.gpsimd
        def _(pool):
            def period(p, par):
                if live(p + 1):
                    pool.wait_ge(s_["hT_hi"], count(p + 1, 1))
                    nc.gpsimd.tensor_tensor(g["hT_lo"][1 - par][:], g["hT"][1 - par][:], g["hT_hi"][1 - par][:].bitcast(F32),
                                            ALU.subtract).then_inc(s_["hT_lo"], 1)
                    pool.wait_ge(s_["xn"], count(p + 1, 4, 3))
                    nc.gpsimd.tensor_tensor(z[:, rows(p + 1), :], z[:, rows(p + 1), :],
                                            g["b_2"][:].unsqueeze(1).broadcast_to([128, TILES, D]), ALU.add).then_inc(s_["zb"], 1)
                if live(p - 2):
                    pool.wait_ge(s_["z_set"], count(p - 2, 1))
                    if live(p - 4):
                        pool.wait_ge(s_["stored"][par], landed(layer * SEQS + p - 4, par))
                    nc.gpsimd.tensor_tensor(g["res"][par][:], z[:, rows(p - 2), :], xa[:, rows(p - 2), :],
                                            ALU.add).then_inc(s_["res"], 1)

            periods(pool, period)

        @block.sync
        def _(sp):
            def period(p, par):
                if live(p - 2):
                    sp.wait_ge(s_["res"], count(p - 2, 1))
                    if live(p - 4):
                        sp.wait_ge(s_["stored"][par], landed(layer * SEQS + p - 4, par))
                    sp.sem_inc(s_["sp_held"], 1)
                    dst = out[bass.ds(p - 2, 1)] if not isinstance(p, int) else out[p - 2:p - 1]
                    sp.dma_start(dst.rearrange("n (t p) d -> p (n t) d", p=128), g["res"][par][:]
                                 ).then_inc(s_["stored"][par], 16)

            periods(sp, period)
            for par in range(2):
                sp.wait_ge(s_["stored"][par], landed(layer * SEQS + SEQS - 2 + par, par))
                sp.sem_inc(s_["sp_held"], 1)

        @block.tensor
        def _(pe):
            def period(p, par):
                if live(p + 1):
                    pe.wait_ge(s_["xn"], count(p + 1, 4, 3))
                    if live(p):
                        pe.wait_ge(s_["hT"], count(p, 3, 2))
                    for i in range(TILES):
                        last = nc.tensor.transpose(bank_t[:, i * 128:(i + 1) * 128], g["xn"][:, i, :], ident[:])
                    last.then_inc(s_["hT_mm"], 1)
                if live(p):
                    pe.wait_ge(s_["hT_lo"], count(p, 1))
                    if live(p - 2):
                        pe.wait_ge(s_["hid"], count(p - 2, 3, 2))
                    hi, lo = g["hT_hi"][par], g["hT_lo"][par]
                    for bank, chunks in ((bank_g[par], (3, 4)), (bank_2[par], (5, 2)), (bank_a[par], (0, 1))):
                        for i, c in enumerate(chunks):
                            dst, w_c = bank[0:HC, i * T:(i + 1) * T], slice(c * HC, (c + 1) * HC)
                            nc.tensor.matmul(dst, g["w_1_hi"][:, w_c], hi[:], start=True, stop=False)
                            nc.tensor.matmul(dst, g["w_1_hi"][:, w_c], lo[:], start=False, stop=False)
                            last = nc.tensor.matmul(dst, g["w_1_lo"][:, w_c], hi[:], start=False, stop=True)
                        last.then_inc(s_["up_mm"], 1)
                if live(p - 1):
                    pe.wait_ge(s_["hid"], count(p - 1, 3, 2))
                    if live(p - 2):
                        pe.wait_ge(s_["z_set"], count(p - 2, 1))
                    for i in range(TILES):
                        for c in range(3):
                            last = nc.tensor.matmul(bank_o[:, i * D:(i + 1) * D], g["hid"][1 - par][:, c, i * 128:(i + 1) * 128],
                                                    g["w_2"][0:HC, c * D:(c + 1) * D], start=(c == 0), stop=(c == 2))
                    last.then_inc(s_["down_mm"], 1)

            periods(pe, period)

        @block.scalar
        def _(act):
            def set_hT(s, par):
                act.wait_ge(s_["hT_mm"], count(s, 1))
                if live(s - 2):
                    act.wait_ge(s_["hT_lo"], count(s - 2, 1))
                for r, dst, src in ((slice(0, 64), slice(0, T), slice(0, T)), (slice(64, 128), slice(1, T), slice(0, T - 1)),
                                    (slice(64, 128), slice(0, 1), slice(T - 1, T))):
                    nc.scalar.activation(g["hT"][par][r, dst], bank_t[r, src], ACT.Identity, scale=g["norm"][r, 0:1],
                                         bias=g["norm"][r, 1:2]).then_inc(s_["hT"], 1)
                act.wait_ge(s_["hT"], count(s, 3, 2))
                if live(s - 2):
                    act.wait_ge(s_["up_mm"], count(s - 2, 3, 2))
                nc.scalar.activation(g["hT_hi"][par][:], g["hT"][par][:], ACT.Copy).then_inc(s_["hT_hi"], 1)

            def gelu(s, par):
                for c in range(3):
                    act.wait_ge(s_["up_mm"], count(s, 3, c // 2))
                    if live(s - 2):
                        act.wait_ge(s_["hid"], count(s - 2, 3, c))
                    src = bank_2[par][0:HC, 0:T] if c == 2 else bank_g[par][0:HC, c * T:(c + 1) * T]
                    nc.scalar.activation(g["gate"][par][:, c, :], src, ACT.Gelu, bias=g["b_1"][0:HC, 3 + c:4 + c]
                                         ).then_inc(s_["gate"], 1)

            def period(p, par):
                if live(p + 1):
                    set_hT(p + 1, 1 - par)
                if live(p):
                    gelu(p, par)

            periods(act, period)

        @block.vector
        def _(dve):
            def period(p, par):
                if live(p - 2):
                    dve.wait_ge(s_["down_mm"], count(p - 2, 1))
                    dve.wait_ge(s_["zb"], count(p - 2, 1))
                    nc.vector.tensor_tensor(z[:, rows(p - 2), :], z[:, rows(p - 2), :],
                                            bank_o[:, 0:T].rearrange("p (t d) -> p t d", d=D), ALU.add).then_inc(s_["z_set"], 1)
                if live(p - 1):
                    q = 1 - par
                    for c in range(3):
                        dve.wait_ge(s_["gate"], count(p - 1, 3, 2))
                        dve.wait_ge(s_["up_mm"], count(p - 1, 3, 2))
                        if live(p - 3):
                            dve.wait_ge(s_["down_mm"], count(p - 3, 1))
                        src = bank_2[q][0:HC, T:2 * T] if c == 2 else bank_a[q][0:HC, c * T:(c + 1) * T]
                        nc.vector.scalar_tensor_tensor(out=g["hid"][q][:, c, :], in0=src, scalar=g["b_1"][0:HC, c:c + 1],
                                                       in1=g["gate"][q][:, c, :], op0=ALU.add, op1=ALU.mult
                                                       ).then_inc(s_["hid"], 1)
                if live(p + 2):
                    if live(p + 1):
                        dve.wait_ge(s_["hT_mm"], count(p + 1, 1))
                    for i in range(TILES):
                        n = (p + 2) * TILES + i
                        for half, v in ((0, rb), (1, rb_next)):
                            f = slice(64 * half, 64 * half + 64)
                            nc.vector.tensor_scalar(g["xn"][:, i, f], z[:, n, f], v[:, 0, i, bass.ds(p + 2, 1)],
                                                    v[:, 1, i, bass.ds(p + 2, 1)], ALU.mult, ALU.add).then_inc(s_["xn"], 1)

            periods(dve, period)


def mlp_buffers(nc, ctx, window):
    def sb(name, shape, dt=F32):
        return ctx.enter_context(nc.sbuf_tensor("c_" + name, shape, dt))

    N = SEQS * TILES
    g = {name: sb(name, shape) for name, shape in dict(
        w_1=[128, 6 * HC], w_2=[128, 3 * D], b_1=[128, 6], norm=[128, 2], b_2=[128, D],
        moved=[128, N, 6], zeros=[1, 64], zero_stats=[1, 6], mv=[128, N, 2], sums=[128, 2, N], dev=[128, N, 4], dev2=[128, N, 4], log_var=[128, TILES, SEQS],
        rb=[128, 2, TILES, SEQS], rb_next=[128, 2, TILES, SEQS], xn=[128, TILES, D],
    ).items()}
    for name, shape in (("hT", [128, T]), ("gate", [HC, 3, T]), ("hid", [HC, 3, T]), ("res", [128, TILES, D])):
        g[name] = [sb(f"{name}{i}", shape) for i in range(2)]
    g["hT_hi"], g["hT_lo"] = window["hT_hi"], window["hT_lo"]
    g["w_1_hi"], g["w_1_lo"] = window["w_qk_hi"][:, 0:6 * HC], window["w_qk_lo"][:, 0:6 * HC]
    names = """w_hi w_lo hT_hi hT_lo w_in zero1 zero_stats stats_in stats_set mv rb rb_r log_var next_in sp_held xn zb z_set stored0 stored1 res hT hT_mm
        hid up_mm down_mm gate""".split()
    g["sems"] = {name: ctx.enter_context(nc.semaphore("c_" + name)) for name in names}
    g["sems"]["stored"] = [g["sems"]["stored0"], g["sems"]["stored1"]]
    return g


def layouts(x):
    bf = np.dtype("bfloat16")
    f = np.float32
    c = {}
    c["ident"] = np.eye(128, dtype=f)
    c["identb"] = np.eye(128, dtype=f).astype(bf)
    mr, k_ones = np.zeros((3 * HA, CHUNKS, 128), f), np.zeros((128, 1), f)
    for part in range(3):
        for h in range(HA):
            mr[part * HA + h, h // 4, 32 * (h % 4) + 3 * DA + part] = 1
            k_ones[32 * (h % 4) + 3 * DA + part] = 1
    c["a_max_rows"], c["a_k_ones"] = mr.astype(bf), k_ones
    wT = np.ascontiguousarray(x["L0_attn_W_qkv"].T)
    swap = np.arange(128) ^ 1
    c["a_w_qk"] = np.stack([wT[:, 0:128], wT[:, 128:256], wT[:, 0:128][:, swap], wT[:, 128:256][:, swap]], 1)
    c["a_w_v"] = wT[:, 256:384]
    woT = x["L0_attn_W_out"].T
    wo = np.zeros((128, CHUNKS, 128), f)
    for h in range(HA):
        wo[32 * (h % 4):32 * (h % 4) + DA, h // 4, :] = woT[DA * h:DA * h + DA, :]
    c["a_w_out"] = wo
    freqs = (1.0 / np.float32(10000.0) ** (np.arange(0, DA, 2, dtype=f) / DA)).astype(f)
    ang = np.outer(np.arange(T, dtype=f), freqs).astype(f)
    cos, sin = np.cos(ang).astype(f), np.sin(ang).astype(f)
    pair = (np.arange(128) % DA) // 2
    rc = cos.T[pair]
    rs = sin.T[pair] * np.where(np.arange(128) % 2 == 0, -1, 1).astype(f)[:, None]
    c["a_rope_c"] = np.stack([rc, rc], 1)
    c["a_rope_s"] = np.stack([rs, rs], 1)
    tri = np.where(np.arange(128)[None, :] > np.arange(128)[:, None], MASKED, 0.0)
    c["a_mask_q"] = np.concatenate([tri, 0 * tri, tri], 1).astype(f)
    sel = np.zeros((128, 2, 2, CHUNKS, 128), f)
    for side, order in enumerate(((0, 0, 1), (0, 1, 0))):
        for h in range(HA):
            for slot, part in enumerate(order):
                for d in range(DA):
                    sel[DA * h + d, side, part, h // 4, 32 * (h % 4) + DA * slot + d] = 1
    c["a_sel"] = sel.reshape(128, -1)
    wqkv = x["L0_ffn_wqkv"]
    inner = HB * DB
    cols = [side * inner + (4 * g + j) * DB + half * 32 + d
            for g in range(2) for side in range(2) for half in range(2) for j in (0, 2, 1, 3) for d in range(32)]
    c["b_w_qk"] = wqkv[:, :, cols]
    c["b_w_v"] = wqkv[:, :, 2 * inner:]
    c["b_w_o"] = x["L0_ffn_wo"].reshape(DEPTH, 4, 128, D).transpose(0, 2, 1, 3).reshape(DEPTH, 128, 4 * D)
    c["b_scales"] = np.stack([np.tile(x[name][:, half * 32:half * 32 + 32], (1, 4))
                              for name in ("L0_ffn_q_scale", "L0_ffn_k_scale") for half in range(2)], 2)
    half_idx = np.arange(0, DB, 2, dtype=f)
    inv_freq = (1.0 / np.float32(10000.0) ** (half_idx / DB)).astype(f)
    pos = np.arange(T, dtype=f)
    ang = (pos[:, None] * inv_freq[None, :]).astype(f)
    base = ((half_idx + np.float32(0.4 * DB)) / np.float32(1.4 * DB)).astype(f)
    power = ((pos - T // 2) / np.float32(WINDOW // 2)).astype(f)
    xpos = (base[None, :] ** power[:, None]).astype(f)
    cos, sin = np.cos(ang).astype(f), np.sin(ang).astype(f)
    tab = [[NORM_SHIFT * QK_SCALE * cos * xpos, NORM_SHIFT * QK_SCALE * sin * xpos],
           [NORM_SHIFT * cos / xpos, NORM_SHIFT * sin / xpos]]
    c["b_rope"] = np.stack([np.stack([np.tile(a.T, (4, 1)) for a in side], 1) for side in tab], 1).astype(f)
    head = np.arange(128) // 32
    hs = np.zeros((128, 32), f)
    hs[np.arange(128), head] = 1
    c["b_head_sum"] = hs
    rep = np.zeros((128, 4, 128), f)
    for u in range(4):
        rep[32 * u + head, u, np.arange(128)] = 1
    c["b_head_rep"] = rep.reshape(128, -1)
    p, n = np.arange(128)[:, None], np.arange(320)[None, :]
    q, k = np.where(n < 128, p, 128 + p), np.where(n < 128, n, n - 64)
    c["b_mask_q"] = np.where((q >= k) & (q <= k + WINDOW), 0.0, MASKED).astype(f)
    q, k = np.where(n < 192, n, n - 64), np.where(n < 192, p, 128 + p)
    c["b_mask_k"] = np.where((q >= k) & (q <= k + WINDOW), 0.0, MASKED).astype(bf)
    hr = np.zeros((3 * HB, HB, 128), f)
    for part in range(3):
        for h in range(HB):
            hr[part * HB + h, h, :] = 1
    c["b_head_row"] = hr.astype(bf)
    def chunked(a, axis):
        pad = [(0, 0)] * a.ndim
        pad[axis] = (0, 3 * HC - HIDDEN)
        return np.pad(a, pad)
    w1, b1, w2 = x["L0_ffn_w1"], x["L0_ffn_b1"], x["L0_ffn_w2"]
    c["c_w_1"] = np.concatenate([chunked(w1[:, :, :HIDDEN], 2), chunked(w1[:, :, HIDDEN:], 2)], 2)
    b = np.concatenate([chunked(b1[:, :HIDDEN], 1), chunked(b1[:, HIDDEN:], 1)], 1).reshape(DEPTH, 6, HC)
    c["c_b_1"] = np.pad(b.transpose(0, 2, 1), ((0, 0), (0, 128 - HC), (0, 0)))
    c["c_w_2"] = np.pad(chunked(w2, 1).reshape(DEPTH, 3, HC, D).transpose(0, 2, 1, 3),
                        ((0, 0), (0, 128 - HC), (0, 0), (0, 0))).reshape(DEPTH, 128, 3 * D)
    c["c_norm"] = np.stack([x["L0_ffn_ln_g"], x["L0_ffn_ln_b"]], 2)
    c["L0_ffn_b2"] = x["L0_ffn_b2"]
    return c


def kernel(**inputs):
    import concourse.bacc as bacc
    from concourse.bass_utils import run_bass_kernel_spmd

    nc = bacc.Bacc("TRN2", target_bir_lowering=False, num_devices=1)
    x = {k: np.ascontiguousarray(v) for k, v in inputs.items()}
    arrays = {"L0_attn_x": x["L0_attn_x"], **layouts(x)}
    arrays = {k + "_dram": np.ascontiguousarray(v) for k, v in arrays.items()}
    t = {k[:-5]: nc.dram_tensor(k, v.shape, mybir.dt.from_np(v.dtype), kind="ExternalInput").ap() for k, v in arrays.items()}
    out = nc.dram_tensor("out", (SEQS, T, D), F32, kind="ExternalOutput").ap()
    build(nc, t, out)
    r = run_bass_kernel_spmd(nc, [arrays], core_ids=[0])
    return r.results[0]["out"]
```
